# Optimizing a Trainium2 kernel written in Bass

```python
import numpy as np
import jax
import jax.numpy as jnp

def _softmax(x, axis=-1):
    return jax.nn.softmax(x, axis=axis)

def _gelu(x):
    return jax.nn.gelu(x, approximate=True)

def _silu(x):
    return jax.nn.silu(x)

def _sigmoid(x):
    return jax.nn.sigmoid(x)

def _layernorm(x, axis=-1, eps=1e-05):
    m = jnp.mean(x, axis=axis, keepdims=True)
    v = jnp.var(x, axis=axis, keepdims=True)
    return (x - m) / jnp.sqrt(v + eps)

def _scatter_add(tgt, idx, src, axis=0):
    return tgt.at[idx].add(src)

def _segment_sum(src, seg, n):
    return jax.ops.segment_sum(src, seg, n)
kernel_name = 'mk_gnn_resnorm_d4_gnn_r8_9f9839'

def setup_inputs(seed: int=0):
    np.random.seed(seed)
    _w = jnp.asarray

    def _rec_inputs():
        import jax
        import jax.numpy as jnp
        _gk = jax.random.key(seed)
        x = -0.0003713 + 1 * jax.random.normal(jax.random.fold_in(_gk, 1), (12500, 128), jnp.float32)
        src = jax.random.randint(jax.random.fold_in(_gk, 2), (200000,), 0, 12500, jnp.int32)
        dst = jax.random.randint(jax.random.fold_in(_gk, 3), (200000,), 0, 12500, jnp.int32)
        _o = jnp.argsort(dst, stable=True)
        src = src[_o]
        dst = dst[_o]
        edge_attr_128 = -5.16925e-05 + 1.00005 * jax.random.normal(jax.random.fold_in(_gk, 12), (200000, 128), jnp.float32)
        edge_type_16 = jax.random.randint(jax.random.fold_in(_gk, 14), (200000,), 0, 16, jnp.int32)
        edge_weight = jax.random.uniform(jax.random.fold_in(_gk, 15), (200000,), jnp.float32, 0.0, 1)
        return (x, src, dst, edge_attr_128, edge_type_16, edge_weight)
    x, src, dst, edge_attr_128, edge_type_16, edge_weight = _rec_inputs()

    def _L0_gnn_setup():
        import jax, jax.numpy as jnp
        import numpy as np
        N = 12500
        E = 80000
        D = 128

        def _weighted_mean_agg(ft, w, src, dst, n_nodes):
            m = ft[src] * w[:, None]
            msum = jax.ops.segment_sum(m, dst, num_segments=n_nodes)
            wsum = jax.ops.segment_sum(w, dst, num_segments=n_nodes)
            safe = jnp.where(wsum > 0, wsum, 1.0)
            return jnp.where((wsum > 0)[:, None], msum / safe[:, None], 0.0)
        key = jax.random.key(seed)
        ks = jax.random.split(key, 10)
        s = 1.0 / np.sqrt(D)
        feat = jax.random.normal(ks[0], (N, D), jnp.float32)
        w = jax.random.uniform(ks[1], (E,), jnp.float32)
        src = jax.random.randint(ks[2], (E,), 0, N, dtype=jnp.int32)
        dst = jax.random.randint(ks[3], (E,), 0, N, dtype=jnp.int32)
        W1 = jax.random.uniform(ks[4], (D, D), jnp.float32, -s, s)
        W2 = jax.random.uniform(ks[5], (D, D), jnp.float32, -s, s)
        sg = 1.0 / np.sqrt(D)
        w_ih = jax.random.uniform(ks[6], (3 * D, 2 * D), jnp.float32, -sg, sg)
        w_hh = jax.random.uniform(ks[7], (3 * D, D), jnp.float32, -sg, sg)
        b_ih = jax.random.uniform(ks[8], (3 * D,), jnp.float32, -sg, sg)
        b_hh = jax.random.uniform(ks[9], (3 * D,), jnp.float32, -sg, sg)
        return {'feat': feat, 'w': w, 'src': src, 'dst': dst, 'W1': W1, 'W2': W2, 'w_ih': w_ih, 'w_hh': w_hh, 'b_ih': b_ih, 'b_hh': b_hh}
    _L0_gnn_all = _L0_gnn_setup()
    _L0_gnn_in = {k: v for k, v in _L0_gnn_all.items() if k in ('W1', 'W2', 'w_ih', 'w_hh', 'b_ih', 'b_hh')}
    del _L0_gnn_all

    def _L1_gnn_setup():
        import jax, jax.numpy as jnp
        import numpy as np
        NUM_NODES = 12500
        NUM_EDGES = 80000
        IN_DIM = 128
        OUT_DIM = 128
        NUM_REL = 16
        key = jax.random.key(seed)
        k1, k2, k3, k4, k5 = jax.random.split(key, 5)
        x = jax.random.normal(k1, (NUM_NODES, IN_DIM), dtype=jnp.float32)
        edge_index = jax.random.randint(k2, (2, NUM_EDGES), 0, NUM_NODES, dtype=jnp.int64)
        edge_types = jax.random.randint(k3, (NUM_EDGES,), 0, NUM_REL, dtype=jnp.int64)
        rw_bound = float(np.sqrt(6.0 / (IN_DIM * OUT_DIM + NUM_REL)))
        relation_weights = jax.random.uniform(k4, (NUM_REL, IN_DIM, OUT_DIM), dtype=jnp.float32, minval=-rw_bound, maxval=rw_bound)
        sw_bound = float(np.sqrt(6.0 / (IN_DIM + OUT_DIM)))
        self_weight = jax.random.uniform(k5, (IN_DIM, OUT_DIM), dtype=jnp.float32, minval=-sw_bound, maxval=sw_bound)
        bias = jnp.zeros((OUT_DIM,), dtype=jnp.float32)
        return {'x': x, 'edge_index': edge_index, 'edge_types': edge_types, 'relation_weights': relation_weights, 'self_weight': self_weight, 'bias': bias}
    _L1_gnn_all = _L1_gnn_setup()
    _L1_gnn_in = {k: v for k, v in _L1_gnn_all.items() if k in ('relation_weights', 'self_weight', 'bias')}
    del _L1_gnn_all

    def _L2_gnn_setup():
        import jax, jax.numpy as jnp
        import numpy as np
        N, E, D = (6250, 100000, 128)
        LN_EPS = 1e-05
        key = jax.random.key(seed)
        ks = jax.random.split(key, 8)
        x = jax.random.normal(ks[0], (N, D), dtype=jnp.float32)
        edge_index = jax.random.randint(ks[1], (2, E), 0, N, dtype=jnp.int64)
        edge_attr = jax.random.normal(ks[2], (E, D), dtype=jnp.float32)
        s_msg = 1.0 / np.sqrt(2 * D)
        s_upd = 1.0 / np.sqrt(2 * D)
        W_msg = jax.random.uniform(ks[3], (2 * D, D), jnp.float32, -s_msg, s_msg)
        b_msg = jax.random.uniform(ks[4], (D,), jnp.float32, -s_msg, s_msg)
        W_upd = jax.random.uniform(ks[5], (2 * D, D), jnp.float32, -s_upd, s_upd)
        b_upd = jax.random.uniform(ks[6], (D,), jnp.float32, -s_upd, s_upd)
        gamma = jnp.ones((D,), jnp.float32)
        beta = jnp.zeros((D,), jnp.float32)
        return {'x': x, 'edge_index': edge_index, 'edge_attr': edge_attr, 'W_msg': W_msg, 'b_msg': b_msg, 'W_upd': W_upd, 'b_upd': b_upd, 'gamma': gamma, 'beta': beta}
    _L2_gnn_all = _L2_gnn_setup()
    _L2_gnn_in = {k: v for k, v in _L2_gnn_all.items() if k in ('W_msg', 'b_msg', 'W_upd', 'b_upd', 'gamma', 'beta')}
    del _L2_gnn_all

    def _L3_gnn_setup():
        import jax, jax.numpy as jnp
        import numpy as np
        N_NODES = 12500
        N_EDGES = 200000
        D = 128

        def _sage_mean(x, src, dst, n, Wl, Wr, b):
            msg = x[src]
            agg = jax.ops.segment_sum(msg, dst, num_segments=n)
            deg = jax.ops.segment_sum(jnp.ones((src.shape[0],), x.dtype), dst, num_segments=n)
            mean = agg / jnp.maximum(deg, 1.0)[:, None]
            return mean @ Wl.T + x @ Wr.T + b
        key = jax.random.key(seed)
        ks = jax.random.split(key, 8)
        s = 1.0 / np.sqrt(D)
        x = jax.random.normal(ks[0], (N_NODES, D), dtype=jnp.float32)
        edge_index = jax.random.randint(ks[1], (2, N_EDGES), 0, N_NODES, dtype=jnp.int64)
        Wl1 = jax.random.normal(ks[2], (D, D), dtype=jnp.float32) * s
        Wr1 = jax.random.normal(ks[3], (D, D), dtype=jnp.float32) * s
        b1 = jax.random.normal(ks[4], (D,), dtype=jnp.float32) * s
        Wl2 = jax.random.normal(ks[5], (D, D), dtype=jnp.float32) * s
        Wr2 = jax.random.normal(ks[6], (D, D), dtype=jnp.float32) * s
        b2 = jax.random.normal(ks[7], (D,), dtype=jnp.float32) * s
        return {'x': x, 'edge_index': edge_index, 'Wl1': Wl1, 'Wr1': Wr1, 'b1': b1, 'Wl2': Wl2, 'Wr2': Wr2, 'b2': b2}
    _L3_gnn_all = _L3_gnn_setup()
    _L3_gnn_in = {k: v for k, v in _L3_gnn_all.items() if k in ('Wl1', 'Wr1', 'b1', 'Wl2', 'Wr2', 'b2')}
    del _L3_gnn_all
    return {'x': x, 'src': src, 'dst': dst, 'edge_attr_128': edge_attr_128, 'edge_type_16': edge_type_16, 'edge_weight': edge_weight, 'L0_gnn_W1': _L0_gnn_in['W1'], 'L0_gnn_W2': _L0_gnn_in['W2'], 'L0_gnn_w_ih': _L0_gnn_in['w_ih'], 'L0_gnn_w_hh': _L0_gnn_in['w_hh'], 'L0_gnn_b_ih': _L0_gnn_in['b_ih'], 'L0_gnn_b_hh': _L0_gnn_in['b_hh'], 'L1_gnn_relation_weights': _L1_gnn_in['relation_weights'], 'L1_gnn_self_weight': _L1_gnn_in['self_weight'], 'L1_gnn_bias': _L1_gnn_in['bias'], 'L2_gnn_W_msg': _L2_gnn_in['W_msg'], 'L2_gnn_b_msg': _L2_gnn_in['b_msg'], 'L2_gnn_W_upd': _L2_gnn_in['W_upd'], 'L2_gnn_b_upd': _L2_gnn_in['b_upd'], 'L2_gnn_gamma': _L2_gnn_in['gamma'], 'L2_gnn_beta': _L2_gnn_in['beta'], 'L3_gnn_Wl1': _L3_gnn_in['Wl1'], 'L3_gnn_Wr1': _L3_gnn_in['Wr1'], 'L3_gnn_b1': _L3_gnn_in['b1'], 'L3_gnn_Wl2': _L3_gnn_in['Wl2'], 'L3_gnn_Wr2': _L3_gnn_in['Wr2'], 'L3_gnn_b2': _L3_gnn_in['b2']}

def reference(x, src, dst, edge_attr_128, edge_type_16, edge_weight, L0_gnn_W1, L0_gnn_W2, L0_gnn_w_ih, L0_gnn_w_hh, L0_gnn_b_ih, L0_gnn_b_hh, L1_gnn_relation_weights, L1_gnn_self_weight, L1_gnn_bias, L2_gnn_W_msg, L2_gnn_b_msg, L2_gnn_W_upd, L2_gnn_b_upd, L2_gnn_gamma, L2_gnn_beta, L3_gnn_Wl1, L3_gnn_Wr1, L3_gnn_b1, L3_gnn_Wl2, L3_gnn_Wr2, L3_gnn_b2):
    import jax
    import jax.numpy as jnp

    def _L0_gnn_ref(feat, w, src, dst, W1, W2, w_ih, w_hh, b_ih, b_hh):
        import jax, jax.numpy as jnp
        import numpy as np
        N = 12500
        E = 80000
        D = 128

        def _weighted_mean_agg(ft, w, src, dst, n_nodes):
            m = ft[src] * w[:, None]
            msum = jax.ops.segment_sum(m, dst, num_segments=n_nodes)
            wsum = jax.ops.segment_sum(w, dst, num_segments=n_nodes)
            safe = jnp.where(wsum > 0, wsum, 1.0)
            return jnp.where((wsum > 0)[:, None], msum / safe[:, None], 0.0)
        n = feat.shape[0]
        neigh1 = _weighted_mean_agg(feat, w, src, dst, n)
        neigh2 = _weighted_mean_agg(feat, w, dst, src, n)
        hn = jnp.concatenate([neigh1 @ W1.T, neigh2 @ W2.T], axis=1)
        gi = hn @ w_ih.T + b_ih
        gh = feat @ w_hh.T + b_hh
        i_r, i_z, i_n = jnp.split(gi, 3, axis=1)
        h_r, h_z, h_n = jnp.split(gh, 3, axis=1)
        r = jax.nn.sigmoid(i_r + h_r)
        z = jax.nn.sigmoid(i_z + h_z)
        nn_ = jnp.tanh(i_n + r * h_n)
        return nn_ + z * (feat - nn_)

    def _L1_gnn_ref(x, edge_index, edge_types, relation_weights, self_weight, bias):
        import jax, jax.numpy as jnp
        import numpy as np
        NUM_NODES = 12500
        NUM_EDGES = 80000
        IN_DIM = 128
        OUT_DIM = 128
        NUM_REL = 16
        num_nodes = x.shape[0]
        self_msg = x @ self_weight
        transformed = jnp.einsum('ni,rio->rno', x, relation_weights)
        src = edge_index[0]
        dst = edge_index[1]
        msgs = transformed[edge_types, src]
        neighbor_msg = jax.ops.segment_sum(msgs, dst, num_segments=num_nodes)
        return jax.nn.relu(self_msg + neighbor_msg + bias)

    def _L2_gnn_ref(x, edge_index, edge_attr, W_msg, b_msg, W_upd, b_upd, gamma, beta):
        import jax, jax.numpy as jnp
        import numpy as np
        N, E, D = (6250, 100000, 128)
        LN_EPS = 1e-05
        src, dst = (edge_index[0], edge_index[1])
        n = x.shape[0]
        msg_in = jnp.concatenate([x[src], edge_attr], axis=-1)
        msg = jax.nn.relu(msg_in @ W_msg + b_msg)
        summed = jax.ops.segment_sum(msg, dst, num_segments=n)
        counts = jax.ops.segment_sum(jnp.ones((msg.shape[0],), x.dtype), dst, num_segments=n)
        mean_msg = summed / jnp.maximum(counts, 1.0)[:, None]
        h = jnp.concatenate([x, mean_msg], axis=-1) @ W_upd + b_upd
        mu = jnp.mean(h, axis=-1, keepdims=True)
        var = jnp.mean(jnp.square(h - mu), axis=-1, keepdims=True)
        h = (h - mu) * jax.lax.rsqrt(var + LN_EPS) * gamma + beta
        return jax.nn.relu(h + x)

    def _L3_gnn_ref(x, edge_index, Wl1, Wr1, b1, Wl2, Wr2, b2):
        import jax, jax.numpy as jnp
        import numpy as np
        N_NODES = 12500
        N_EDGES = 200000
        D = 128

        def _sage_mean(x, src, dst, n, Wl, Wr, b):
            msg = x[src]
            agg = jax.ops.segment_sum(msg, dst, num_segments=n)
            deg = jax.ops.segment_sum(jnp.ones((src.shape[0],), x.dtype), dst, num_segments=n)
            mean = agg / jnp.maximum(deg, 1.0)[:, None]
            return mean @ Wl.T + x @ Wr.T + b
        src, dst = (edge_index[0], edge_index[1])
        n = x.shape[0]
        h = _sage_mean(x, src, dst, n, Wl1, Wr1, b1)
        h = jax.nn.relu(h)
        return _sage_mean(h, src, dst, n, Wl2, Wr2, b2)
    edge_index = jnp.stack([src, dst])
    x = _layernorm(x + _L0_gnn_ref(x, edge_weight, src, dst, L0_gnn_W1, L0_gnn_W2, L0_gnn_w_ih, L0_gnn_w_hh, L0_gnn_b_ih, L0_gnn_b_hh), axis=-1)
    x = _layernorm(x + _L1_gnn_ref(x, edge_index, edge_type_16, L1_gnn_relation_weights, L1_gnn_self_weight, L1_gnn_bias), axis=-1)
    x = _layernorm(x + _L2_gnn_ref(x, edge_index, edge_attr_128, L2_gnn_W_msg, L2_gnn_b_msg, L2_gnn_W_upd, L2_gnn_b_upd, L2_gnn_gamma, L2_gnn_beta), axis=-1)
    x = _layernorm(x + _L3_gnn_ref(x, edge_index, L3_gnn_Wl1, L3_gnn_Wr1, L3_gnn_b1, L3_gnn_Wl2, L3_gnn_Wr2, L3_gnn_b2), axis=-1)
    return x

_drawn_inputs = setup_inputs


def setup_inputs(seed=0):
    import zlib

    import numpy as np

    out = dict(_drawn_inputs(seed))
    spreads = {'L1_gnn_bias': (0.0, 0.1), 'L2_gnn_gamma': (1.0, 0.2), 'L2_gnn_beta': (0.0, 0.1)}
    factors = {'L0_gnn_b_hh': 4.021, 'L2_gnn_b_msg': 6.92}
    for name, (base, spread) in spreads.items():
        noise = np.random.default_rng([zlib.crc32(name.encode()), seed]).standard_normal(out[name].shape)
        drawn = base * np.exp(spread * noise) if base else spread * noise
        out[name] = jnp.asarray(drawn.astype(out[name].dtype))
    for name, factor in factors.items():
        out[name] = (out[name] * factor).astype(out[name].dtype)
    return out
```

```python
from contextlib import ExitStack

import numpy as np

import concourse.bass as bass
from concourse import mybir

F32 = mybir.dt.float32
I32 = mybir.dt.int32
ALU = mybir.AluOpType
ACT = mybir.ActivationFunctionType
AX = mybir.AxisListType
ds = bass.ds


class Memory:
    pass


class Step:
    pass


class TileProgram:

    def __init__(self, credits, sp, sp_end, dve, act, pe):
        self.credits, self.sp, self.sp_end, self.dve, self.act, self.pe = credits, sp, sp_end, dve, act, pe


P = 128
N = 12500
E = 200000
D = 128
R = 16
NT = -(-N // P)
NPAD = NT * P
NC = -(-E // P)
SLOTS = 16
QUAD = 4
NQ = SLOTS // QUAD
GROUPS = -(-(NC + NT - 1) // SLOTS)
ITEMS = GROUPS * SLOTS
JC = ITEMS // P
W1 = D + 1
NTAB = 8
TRASH = NPAD
TROWS = NPAD + P
NO_NODE = 1 << 20
EPS = 1e-5
assert ITEMS % P == 0 and JC * P == ITEMS

C_ID, C_IOTA, C_LOW, C_K, C_TRASH, C_BOUND = 0, P, 2 * P, 3 * P, 3 * P + JC, 3 * P + JC + 1
C_TAB = C_BOUND + 1
C_W = C_TAB + NTAB


def constants():
    c = np.zeros((P, C_W), np.float32)
    c[:, C_ID:C_ID + P] = np.eye(P)
    c[:, C_IOTA:C_IOTA + P] = np.arange(P)[None, :]
    c[:, C_LOW:C_LOW + P] = np.tril(np.ones((P, P)), -1)
    c[:, C_K:C_K + JC] = np.arange(JC)[None, :] * P + np.arange(P)[:, None]
    c[:, C_TRASH] = TRASH + np.arange(P)
    c[:, C_BOUND] = P * np.arange(P)
    c[:, C_TAB:C_TAB + NTAB] = TROWS * np.arange(NTAB)[None, :]
    return c


def column(ap, n):
    return ap.to_broadcast([P, n])



def plan_phase(nc, m, d):
    with ExitStack() as ctx:
        def sb(name, shape, dt=F32):
            return ctx.enter_context(nc.sbuf_tensor(name, shape, dt))

        def ps(name):
            return ctx.enter_context(nc.psum_tensor(name, [P, 512], F32))

        def sem(name):
            return ctx.enter_context(nc.semaphore(name))

        firsts_i = sb("firsts_i", [P, NC + 1], I32)
        firsts = sb("firsts", [P, NC + 1])
        below = sb("below", [P, NC + 1])
        nfirst = sb("nfirst", [P, 1])
        lastrow = sb("lastrow", [P, 1])
        lastrow_i = sb("lastrow_i", [P, 1], I32)
        drow_i = sb("drow_i", [P, P], I32)
        drow = sb("drow", [P, P])
        inrow = sb("inrow", [P, 1])
        start_col = sb("start_col", [P, 1])
        start = sb("start", [P, P])
        lo_i = sb("lo_i", [P, NT], I32)
        lo_s = sb("lo_s", [P, NT], I32)
        lo = sb("lo", [P, NT])
        hi_f = sb("hi_f", [P, NT])
        hi_i = sb("hi_i", [P, NT], I32)
        hi_s = sb("hi_s", [P, NT], I32)
        hi = sb("hi", [P, NT])
        some = sb("some", [P, NT])
        cnt = sb("cnt", [P, NT])
        one = sb("one", [P, NT])
        incl = sb("incl", [P, NT])
        first = sb("first", [P, NT])
        g = sb("g", [P, NT])
        dg = sb("dg", [P, NT])
        mask = sb("mask", [P, 2, NT])
        ntile = sb("ntile", [P, JC])
        goff = sb("goff", [P, JC])
        valid = sb("valid", [P, JC])
        chunk = sb("chunk", [P, JC])
        tile = sb("tile", [P, JC])
        base = sb("base", [P, JC])
        chunk_i = sb("chunk_i", [P, JC], I32)
        rows_i = sb("rows_i", [P, JC, 3 * P], I32)
        rows_w = sb("rows_w", [P, JC, P])
        rows = sb("rows", [P, 4, JC, P])
        tc_i = sb("tc_i", [2 * JC, P], I32)
        w1 = sb("w1", [P, P])
        w2 = sb("w2", [P, P])
        wih = sb("wih", [P, 2, 3 * D])
        pa, pb, pc, pd = ps("pa"), ps("pb"), ps("pc"), ps("pd")

        load_firsts, load_const, load_x, load_w = sem("load_firsts"), sem("load_const"), sem("load_x"), sem("load_w")
        chain, act_chain = sem("plan_chain"), sem("act_chain")
        row_idx, row_in, start_ps, start_sb = sem("row_idx"), sem("row_in"), sem("start_ps"), sem("start_sb")
        chunk_ready, rows_in, rows_ready, rows_tp, rows_done = (sem("chunk_ready"), sem("rows_in"), sem("rows_ready"),
                                                                 sem("rows_tp"), sem("rows_done"))
        tc_ready, tc_ps, tc_sb, tc_dram, tc_row = sem("tc_ready"), sem("tc_ps"), sem("tc_sb"), sem("tc_dram"), sem("tc_row")
        fold_ps, fold_sb = sem("fold_ps"), sem("fold_sb")
        tcol = sb("tcol", [P, 2, JC])
        consts = m.consts
        block = ctx.enter_context(nc.Block())

        @block.sync
        def _(sp):
            sp.dma_start(firsts_i[:], d["first_dst"].partition_broadcast(P)).then_inc(load_firsts, 16)
            sp.dma_start(consts[:], d["consts"]).then_inc(load_const, 16)
            sp.dma_start(w1[:], d["L0_gnn_W1"]).then_inc(load_w, 16)
            sp.dma_start(w2[:], d["L0_gnn_W2"]).then_inc(load_w, 16)
            sp.dma_start(wih[:], d["w_ih_t"].rearrange("(h p) g -> p h g", h=2)).then_inc(load_w, 16)
            sp.dma_start(m.x[:, :, 0:D], d["x_pad"].rearrange("(t p) f -> p t f", p=P)).then_inc(load_x, 16)
            loads = [(m.whh[:], d["w_hh_t"]), (m.b_ih[:], d["b_ih"]), (m.b_hh[:], d["b_hh"]), (m.rel[:], d["rel_t"]),
                     (m.selfw[:], d["L1_gnn_self_weight"]), (m.b1[:], d["L1_bias"]),
                     (m.wmsg[:], d["L2_gnn_W_msg"].rearrange("(h p) o -> p h o", h=2)), (m.b_msg[:], d["b_msg"]),
                     (m.wupd[:], d["L2_gnn_W_upd"].rearrange("(h p) o -> p h o", h=2)), (m.b_upd[:], d["b_upd"]),
                     (m.gamma[:], d["gamma"].partition_broadcast(P)), (m.beta[:], d["beta"].partition_broadcast(P)),
                     (m.wl1[:], d["wl1_t"]), (m.wr1[:], d["wr1_t"]), (m.b31[:], d["b31"]),
                     (m.wl2[:], d["wl2_t"]), (m.wr2[:], d["wr2_t"]), (m.b32[:], d["b32"])]
            for to, src in loads:
                sp.dma_start(to, src).then_inc(load_x, 16)
            sp.wait_ge(tc_sb, 1)
            sp.dma_start(d["tc_dram"], tc_i[:]).then_inc(tc_dram, 16)
            sp.wait_ge(tc_dram, 16)
            sp.dma_start(m.item_tc[:], d["tc_dram"].rearrange("(a b) p -> a (b p)", a=1)).then_inc(tc_row, 16)
            sp.wait_ge(tc_row, 16)
            sp.wait_ge(load_x, 16 * (1 + len(loads)))

        @block.gpsimd
        def _(pool):
            pool.memset(m.ones[:], 1.0)
            pool.memset(m.zeros[:], 0.0)
            pool.memset(m.eps[:], EPS)
            pool.memset(m.x[:, :, D:W1], 1.0)
            pool.wait_ge(row_idx, 1)
            pool.indirect_dma_start(out=drow_i[:], out_offset=None, in_=d["dst_rows"],
                                    in_offset=bass.IndirectOffsetOnAxis(ap=lastrow_i[:], axis=0)).then_inc(row_in, 16)
            pool.wait_ge(chunk_ready, 1)
            for j in range(JC):
                pool.indirect_dma_start(out=rows_i[:, j, :], out_offset=None, in_=d["edge_rows"],
                                        in_offset=bass.IndirectOffsetOnAxis(ap=chunk_i[:, j:j + 1], axis=0)).then_inc(rows_in, 16)
                pool.indirect_dma_start(out=rows_w[:, j, :], out_offset=None, in_=d["weight_rows"],
                                        in_offset=bass.IndirectOffsetOnAxis(ap=chunk_i[:, j:j + 1], axis=0)).then_inc(rows_in, 16)

        @block.vector
        def _(dve):
            n = [0]

            def link(ins):
                n[0] += 1
                ins.then_inc(chain, 1)
                dve.wait_ge(chain, n[0])

            v = nc.vector
            k = consts[:, C_K:C_K + JC]
            bound = consts[:, C_BOUND:C_BOUND + 1]
            dve.wait_ge(load_firsts, 16)
            link(v.tensor_copy(firsts[:], firsts_i[:]))
            dve.wait_ge(load_const, 16)
            link(v.tensor_scalar(below[:], firsts[:], bound, None, op0=ALU.is_lt, op1=ALU.add, accum_out=nfirst[:]))
            link(v.tensor_scalar(lastrow[:], nfirst[:], -1.0, 0.0, op0=ALU.add, op1=ALU.max))
            v.tensor_copy(lastrow_i[:], lastrow[:]).then_inc(row_idx, 1)
            dve.wait_ge(row_in, 16)
            link(v.tensor_copy(drow[:], drow_i[:]))
            link(v.tensor_scalar(below[:, 0:P], drow[:], bound, None, op0=ALU.is_lt, op1=ALU.add, accum_out=inrow[:]))
            v.scalar_tensor_tensor(start_col[:], lastrow[:], float(P), inrow[:], ALU.mult, ALU.add).then_inc(start_sb, 1)
            dve.wait_ge(start_ps, 1)
            link(v.tensor_copy(start[:], pa[:, 0:P]))
            link(v.tensor_copy(lo_i[:], start[:, 0:NT]))
            link(v.tensor_scalar(lo_s[:], lo_i[:], 7, None, op0=ALU.arith_shift_right))
            link(v.tensor_copy(lo[:], lo_s[:]))
            link(v.tensor_scalar_add(hi_f[:], start[:, 1:NT + 1], float(P - 1)))
            link(v.tensor_copy(hi_i[:], hi_f[:]))
            link(v.tensor_scalar(hi_s[:], hi_i[:], 7, None, op0=ALU.arith_shift_right))
            link(v.tensor_copy(hi[:], hi_s[:]))
            link(v.tensor_tensor(some[:], start[:, 1:NT + 1], start[:, 0:NT], ALU.is_gt))
            link(v.tensor_tensor(cnt[:], hi[:], lo[:], ALU.subtract))
            link(v.tensor_tensor(cnt[:], cnt[:], some[:], ALU.mult))
            link(v.memset(one[:], 1.0))
            link(v.tensor_tensor_scan(incl[:], one[:], cnt[:], 0.0, ALU.mult, ALU.add))
            link(v.tensor_tensor(first[:], incl[:], cnt[:], ALU.subtract))
            link(v.tensor_tensor(g[:], lo[:], first[:], ALU.subtract))
            link(v.tensor_copy(dg[:, 0:1], g[:, 0:1]))
            link(v.tensor_tensor(dg[:, 1:NT], g[:, 1:NT], g[:, 0:NT - 1], ALU.subtract))
            for j in range(JC):
                link(v.tensor_scalar(mask[:, 0, :], first[:], k[:, j:j + 1], None, op0=ALU.is_le, op1=ALU.add,
                                     accum_out=ntile[:, j:j + 1]))
                link(v.scalar_tensor_tensor(mask[:, 1, :], first[:], k[:, j:j + 1], dg[:], ALU.is_le, ALU.mult,
                                            accum_out=goff[:, j:j + 1]))
            link(v.tensor_scalar(valid[:], k, incl[:, NT - 1:NT], None, op0=ALU.is_lt))
            link(v.tensor_scalar_add(tile[:], ntile[:], -1.0))
            link(v.tensor_tensor(chunk[:], k, goff[:], ALU.add))
            link(v.scalar_tensor_tensor(chunk[:], chunk[:], -float(NC), valid[:], ALU.add, ALU.mult))
            link(v.tensor_scalar_add(chunk[:], chunk[:], float(NC)))
            v.tensor_copy(chunk_i[:], chunk[:]).then_inc(chunk_ready, 1)
            link(v.tensor_copy(tcol[:, 0, :], tile[:]))
            v.tensor_copy(tcol[:, 1, :], chunk[:]).then_inc(tc_ready, 1)
            link(v.tensor_scalar_mul(base[:], tile[:], float(P)))
            dve.wait_ge(tc_ps, 1)
            v.tensor_copy(tc_i[:], pb[0:2 * JC, 0:P]).then_inc(tc_sb, 1)
            dve.wait_ge(rows_in, 16 * 2 * JC)
            link(v.tensor_copy(rows[:, 0, :, :], rows_i[:, :, 0:P]))
            link(v.tensor_copy(rows[:, 1, :, :], rows_i[:, :, P:2 * P]))
            link(v.tensor_tensor(rows[:, 1, :, :], rows[:, 1, :, :],
                                 base[:].unsqueeze(2).to_broadcast([P, JC, P]), ALU.subtract))
            link(v.tensor_copy(rows[:, 2, :, :], rows_w[:]))
            link(v.tensor_copy(rows[:, 3, :, :], rows_i[:, :, 2 * P:3 * P]))
            v.scalar_tensor_tensor(rows[:, 3, :, :], rows[:, 0, :, :], float(R), rows[:, 3, :, :],
                                   ALU.mult, ALU.add).then_inc(rows_ready, 1)

        @block.tensor
        def _(pe):
            ident = consts[:, C_ID:C_ID + P]
            pe.wait_ge(load_const, 16)
            pe.wait_ge(load_w, 48)
            nc.tensor.matmul(pc[:, 0:3 * D], w1[:], wih[:, 0, :], start=True, stop=True).then_inc(fold_ps, 1)
            nc.tensor.matmul(pd[:, 0:3 * D], w2[:], wih[:, 1, :], start=True, stop=True).then_inc(fold_ps, 1)
            pe.wait_ge(start_sb, 1)
            nc.tensor.matmul(pa[:, 0:P], column(start_col[:], P), ident, start=True, stop=True).then_inc(start_ps, 1)
            pe.wait_ge(tc_ready, 1)
            nc.tensor.transpose(pb[0:2 * JC, 0:P], tcol[:].rearrange("p a j -> p (a j)"), ident).then_inc(tc_ps, 1)
            pe.wait_ge(rows_ready, 1)
            pe.wait_ge(fold_sb, 1)
            for j in range(JC):
                if j:
                    pe.wait_ge(rows_done, j)
                for a in range(4):
                    last = nc.tensor.transpose(pc[:, a * P:(a + 1) * P], rows[:, a, j, :], ident)
                last.then_inc(rows_tp, 1)

        @block.scalar
        def _(act):
            act.wait_ge(fold_ps, 2)
            nc.scalar.activation(m.fold[:, 0, :], pc[:, 0:3 * D], ACT.Copy)
            nc.scalar.activation(m.fold[:, 1, :], pd[:, 0:3 * D], ACT.Copy).then_inc(fold_sb, 1)
            with act.Fori(0, JC) as j:
                act.wait_ge(rows_tp, j + 1)
                act.nop(nofuse=True)
                nc.scalar.activation(m.items[:, :, ds(j * P, P)], pc[:].rearrange("p (a b) -> p a b", a=4),
                                     ACT.Copy).then_inc(rows_done, 1)



def scatter_phase(nc, m, d):
    with ExitStack() as ctx:
        def sb(name, shape, dt=F32):
            return ctx.enter_context(nc.sbuf_tensor(name, shape, dt))

        def ps(name, n):
            return ctx.enter_context(nc.psum_tensor(name, [P, n, 512], F32))

        def sem(name):
            return ctx.enter_context(nc.semaphore(name))

        src_row, ps_m, ps_z = ps("ps_src", 2), ps("ps_m", 2), ps("ps_z", 4)
        ohw = sb("ohw", [P, 2, QUAD, P])
        same = sb("same", [P, 2, QUAD, P])
        tmp = sb("tmp", [P, QUAD, P])
        dup = sb("dup", [P, QUAD])
        away = sb("away", [P, QUAD])
        m_sb = sb("m_sb", [P, 2, QUAD, P])
        z_sb = sb("z_sb", [P, SLOTS, W1])
        ix = sb("ix", [P, SLOTS], I32)
        src_col = sb("src_col", [P, 2, QUAD])
        src_ready = sem("src_ready")
        tables_zero, rows_ps, same_ready, idx_ready, m_ps, m_ready, z_ps, z_ready = (
            sem("tables_zero"), sem("rows_ps"), sem("same_ready"), sem("idx_ready"),
            sem("m_ps"), sem("m_ready"), sem("z_ps"), sem("z_ready"))
        ohw_done, chain = sem("ohw_done"), sem("b_chain")
        freed = sem("freed")
        landed = [sem(f"landed{q}") for q in range(NQ)]
        block = ctx.enter_context(nc.Block())
        K = 5

        @block.sync
        def _(sp):
            rows = TROWS // P
            zp = m.zeros[:].unsqueeze(1).to_broadcast([P, rows, W1])
            for k in range(NTAB):
                sp.dma_start(d["tables"][k * TROWS:(k + 1) * TROWS, :].rearrange("(p r) f -> p r f", p=P), zp).then_inc(tables_zero, 16)
            sp.sem_inc(m_ready, 2)
            sp.sem_inc(z_ready, 2)
            sp.sem_inc(freed, NQ)
            with sp.Fori(0, GROUPS) as j:
                for q in range(NQ):
                    sp.wait_ge(landed[q], (j + 1) * (QUAD * 16))
                    sp.nop(nofuse=True)
                    sp.sem_inc(freed, 1)

        @block.gpsimd
        def _(pool):
            pool.memset(m.acc[:], 0.0)
            pool.wait_ge(tables_zero, 16 * NTAB)
            with pool.Fori(0, GROUPS) as j:
                for q in range(NQ):
                    pool.wait_ge(freed, j * NQ + q + NQ - 1)
                    pool.wait_ge(idx_ready, j * NQ + q + 1)
                    pool.wait_ge(z_ready, j * NQ + q + 1 + 2)
                    pool.nop(nofuse=True)
                    for i in range(QUAD):
                        s = q * QUAD + i
                        pool.indirect_dma_start(
                            out=d["tables"], out_offset=bass.IndirectOffsetOnAxis(ap=ix[:, s:s + 1], axis=0),
                            in_=z_sb[:, s, :], in_offset=None, compute_op=ALU.add).then_inc(landed[q], 16)
            for q in range(NQ):
                pool.wait_ge(landed[q], GROUPS * QUAD * 16)

        @block.vector
        def _(dve):
            v = nc.vector
            iota = m.consts[:, C_IOTA:C_IOTA + P]
            low = m.consts[:, C_LOW:C_LOW + P]
            trash = m.consts[:, C_TRASH:C_TRASH + 1]
            with dve.Fori(0, GROUPS) as j:
                for q in range(NQ):
                    b = q % 2
                    t = j * NQ + q

                    def link(ins, n):
                        ins.then_inc(chain, 1)
                        dve.wait_ge(chain, t * K + n)

                    k0 = j * SLOTS + q * QUAD
                    dve.wait_ge(m_ready, t + 1)
                    v.tensor_scalar_mul(src_col[:, b, :], m.items[:, 0, ds(k0, QUAD)], 1.0).then_inc(src_ready, 1)
                    for i in range(QUAD):
                        v.tensor_scalar(ohw[:, b, i, :], iota, m.items[:, 1, ds(k0 + i, 1)], m.items[:, 2, ds(k0 + i, 1)],
                                        op0=ALU.is_equal, op1=ALU.mult)
                    dve.wait_ge(rows_ps, t + 1)
                    src = m.items[:, 0, ds(k0, QUAD)].unsqueeze(2).to_broadcast([P, QUAD, P])
                    v.tensor_tensor(same[:, b], src_row[:, b, :].rearrange("p (i e) -> p i e", i=QUAD), src,
                                    ALU.is_equal).then_inc(same_ready, 1)
                    dve.wait_ge(same_ready, t + 1)
                    link(v.tensor_tensor(tmp[:], same[:, b], low.unsqueeze(1).to_broadcast([P, QUAD, P]), ALU.mult), 1)
                    link(v.tensor_reduce(dup[:], tmp[:], AX.X, ALU.add), 2)
                    link(v.tensor_scalar(away[:], m.items[:, 0, ds(k0, QUAD)], -1.0, trash, op0=ALU.mult, op1=ALU.add), 3)
                    link(v.scalar_tensor_tensor(away[:], dup[:], 0.0, away[:], ALU.is_gt, ALU.mult), 4)
                    dve.wait_ge(freed, t + 1)
                    link(v.tensor_tensor(away[:], away[:], m.items[:, 0, ds(k0, QUAD)], ALU.add), 5)
                    k = q * QUAD % NTAB
                    v.tensor_tensor(ix[:, q * QUAD:(q + 1) * QUAD], away[:], m.consts[:, C_TAB + k:C_TAB + k + QUAD],
                                    ALU.add).then_inc(idx_ready, 1)

        @block.tensor
        def _(pe):
            ident = m.consts[:, C_ID:C_ID + P]
            with pe.Fori(0, GROUPS) as j:
                for q in range(NQ):
                    b = q % 2
                    t = j * NQ + q
                    k0 = j * SLOTS + q * QUAD
                    pe.wait_ge(src_ready, t + 1)
                    for i in range(QUAD):
                        last = nc.tensor.matmul(src_row[:, b, i * P:(i + 1) * P], column(src_col[:, b, i:i + 1], P),
                                                ident, start=True, stop=True)
                    last.then_inc(rows_ps, 1)
                    pe.wait_ge(same_ready, t + 1)
                    for i in range(QUAD):
                        last = nc.tensor.matmul(ps_m[:, b, i * P:(i + 1) * P], ohw[:, b, i, :], same[:, b, i, :],
                                                start=True, stop=True)
                    last.then_inc(m_ps, 1)
                    pe.wait_ge(m_ready, t + 1 + 2)
                    pe.wait_ge(z_ready, t + 1)
                    for i in range(QUAD):
                        tile = pe.value_load(m.item_tc[0:1, ds(k0 + i, 1)], min_val=0, max_val=NT - 1)
                        last = nc.tensor.matmul(ps_z[:, 2 * b + i // 2, (i % 2) * W1:(i % 2 + 1) * W1], m_sb[:, b, i, :],
                                                m.x[:, ds(tile, 1), :].rearrange("p a f -> p (a f)"), start=True, stop=True)
                    last.then_inc(z_ps, 1)

        @block.scalar
        def _(act):
            with act.Fori(0, GROUPS) as j:
                for q in range(NQ):
                    b = q % 2
                    t = j * NQ + q
                    act.wait_ge(m_ps, t + 1)
                    nc.scalar.activation(m_sb[:, b].rearrange("p i e -> p (i e)"), ps_m[:, b, :], ACT.Copy).then_inc(m_ready, 1)
                    act.wait_ge(z_ps, t + 1)
                    act.wait_ge(freed, t + 1)
                    nc.scalar.activation(z_sb[:, q * QUAD:(q + 1) * QUAD, :].rearrange("p (h i) f -> p h (i f)", h=2),
                                         ps_z[:, 2 * b:2 * b + 2, 0:2 * W1], ACT.Copy).then_inc(z_ready, 1)



def gather_phase(nc, m, d, name, table, idx_row, weighted, edge_mlp):
    with ExitStack() as ctx:
        def sb(nm, shape, dt=F32):
            return ctx.enter_context(nc.sbuf_tensor(f"{name}_{nm}", shape, dt))

        def sem(nm):
            return ctx.enter_context(nc.semaphore(f"{name}_{nm}"))

        rows = sb("rows", [P, SLOTS, W1])
        oh = sb("oh", [P, SLOTS, P])
        ix = sb("ix", [P, SLOTS], I32)
        psum = ctx.enter_context(nc.psum_tensor(f"{name}_sum", [P, QUAD, 512], F32))
        ix_ready, oh_ready, summed, added = sem("ix_ready"), sem("oh_ready"), sem("summed"), sem("added")
        gathered = [sem(f"gathered{q}") for q in range(NQ)]
        if edge_mlp:
            attr = sb("attr", [P, SLOTS, P])
            msg = sb("msg", [P, SLOTS, W1])
            ps_msg = ctx.enter_context(nc.psum_tensor(f"{name}_msg_bank", [P, 2, 512], F32))
            msg_ps, msg_ready = sem("msg_ps"), sem("msg_ready")
            attr_in = [sem(f"attr_in{q}") for q in range(NQ)]
        ones_ready = sem("ones_ready")
        block = ctx.enter_context(nc.Block())

        @block.sync
        def _(sp):
            sp.sem_inc(summed, SLOTS)
            sp.sem_inc(added, QUAD)
            if edge_mlp:
                sp.sem_inc(msg_ready, 2)
                with sp.Fori(0, GROUPS) as j:
                    for q in range(NQ):
                        sp.wait_ge(summed, j * SLOTS + (q + 1) * QUAD)
                        sp.nop(nofuse=True)
                        for i in range(QUAD):
                            s = q * QUAD + i
                            chunk = sp.value_load(m.item_tc[0:1, ds(ITEMS + j * SLOTS + s, 1)], min_val=0, max_val=NC)
                            sp.dma_start(attr[:, s, :], d["attr_t"][ds(chunk, 1), :, :].rearrange("c f e -> (c f) e")
                                         ).then_inc(attr_in[q], 16)

        @block.gpsimd
        def _(pool):
            pool.memset((msg if edge_mlp else rows)[:, :, D:W1], 1.0).then_inc(ones_ready, 1)
            with pool.Fori(0, GROUPS) as j:
                for q in range(NQ):
                    pool.wait_ge(ix_ready, j * NQ + q + 1)
                    pool.nop(nofuse=True)
                    for i in range(QUAD):
                        s = q * QUAD + i
                        pool.indirect_dma_start(out=rows[:, s, 0:D], out_offset=None, in_=table,
                                                in_offset=bass.IndirectOffsetOnAxis(ap=ix[:, s:s + 1], axis=0)
                                                ).then_inc(gathered[q], 16)

        def relu_quad(act, t, q):
            act.wait_ge(msg_ps, t + 1)
            nc.scalar.activation(msg[:, q * QUAD:(q + 1) * QUAD, 0:D],
                                 ps_msg[:, q % 2, :].rearrange("p (i f) -> p i f", i=QUAD), ACT.Relu).then_inc(msg_ready, 1)

        @block.scalar
        def _(act):
            with act.Fori(0, GROUPS) as j:
                for q in range(NQ):
                    act.wait_ge(summed, j * SLOTS + (q + 1) * QUAD)
                    act.nop(nofuse=True)
                    nc.scalar.activation(ix[:, q * QUAD:(q + 1) * QUAD], m.items[:, idx_row, ds(j * SLOTS + q * QUAD, QUAD)],
                                         ACT.Copy).then_inc(ix_ready, 1)
                    if edge_mlp and q >= 2:
                        relu_quad(act, j * NQ + q - 2, q - 2)
                if edge_mlp:
                    relu_quad(act, j * NQ + 2, 2)
                    relu_quad(act, j * NQ + 3, 3)

        @block.vector
        def _(dve):
            v = nc.vector
            iota = m.consts[:, C_IOTA:C_IOTA + P]
            with dve.Fori(0, GROUPS) as j:
                for q in range(NQ):
                    dve.wait_ge(summed, j * SLOTS + (q + 1) * QUAD)
                    for i in range(QUAD):
                        s = q * QUAD + i
                        k = j * SLOTS + s
                        if weighted:
                            v.tensor_scalar(oh[:, s, :], iota, m.items[:, 1, ds(k, 1)], m.items[:, 2, ds(k, 1)],
                                            op0=ALU.is_equal, op1=ALU.mult).then_inc(oh_ready, 1)
                        else:
                            v.tensor_scalar(oh[:, s, :], iota, m.items[:, 1, ds(k, 1)], None,
                                            op0=ALU.is_equal).then_inc(oh_ready, 1)
                    tiles = [dve.value_load(m.item_tc[0:1, ds(j * SLOTS + q * QUAD + i, 1)], min_val=0, max_val=NT - 1)
                             for i in range(QUAD)]
                    for i in range(QUAD):
                        k = j * SLOTS + q * QUAD + i
                        a = m.acc[:, ds(tiles[i], 1), :].rearrange("p a f -> p (a f)")
                        dve.wait_ge(summed, SLOTS + k + 1)
                        dve.wait_ge(added, QUAD + k)
                        v.tensor_tensor(a, a, psum[:, i, 0:W1], ALU.add).then_inc(added, 1)

        @block.tensor
        def _(pe):
            ident = m.consts[:, C_ID:C_ID + P]
            pe.wait_ge(ones_ready, 1)
            with pe.Fori(0, GROUPS) as j:
                for q in range(NQ):
                    pe.wait_ge(gathered[q], (j + 1) * (QUAD * 16))
                    if edge_mlp:
                        pe.wait_ge(attr_in[q], (j + 1) * (QUAD * 16))
                        pe.wait_ge(msg_ready, j * NQ + q + 1)
                        for i in range(QUAD):
                            s = q * QUAD + i
                            o = ps_msg[:, q % 2, i * P:(i + 1) * P]
                            nc.tensor.matmul(o, attr[:, s, :], m.wmsg[:, 1, :], start=True, stop=False)
                            last = nc.tensor.matmul(o, ident, rows[:, s, 0:D], start=False, stop=True)
                        last.then_inc(msg_ps, 1)
                        pe.wait_ge(msg_ready, 2 + j * NQ + q + 1)
                    for i in range(QUAD):
                        s = q * QUAD + i
                        pe.wait_ge(oh_ready, j * SLOTS + s + 1)
                        pe.wait_ge(added, j * SLOTS + s + 1)
                        nc.tensor.matmul(psum[:, i, 0:W1], oh[:, s, :], (msg if edge_mlp else rows)[:, s, :],
                                         start=True, stop=True).then_inc(summed, 1)



class Chain:

    def __init__(self, eng, sem, t, steps):
        self.eng, self.sem, self.base, self.steps, self.n = eng, sem, t * steps, steps, 0

    def link(self, ins):
        self.n += 1
        ins.then_inc(self.sem, 1)
        self.eng.wait_ge(self.sem, self.base + self.n)

    def end(self):
        assert self.n == self.steps, self.n


def tile_of(a, t, n=D):
    return a[:, ds(t, 1), 0:n].rearrange("p a f -> p (a f)")


def tile_phase(nc, m, d, name, steps, body):
    with ExitStack() as ctx:
        s = Step()
        s.sb = lambda nm, shape, dt=F32: ctx.enter_context(nc.sbuf_tensor(f"{name}_{nm}", shape, dt))
        s.sem = lambda nm: ctx.enter_context(nc.semaphore(f"{name}_{nm}"))
        s.bank = [ctx.enter_context(nc.psum_tensor(f"{name}_bank{i}", [P, 512], F32)) for i in range(4)]
        s.chain, s.steps = s.sem("chain"), steps
        p = body(nc, m, d, s)
        block = ctx.enter_context(nc.Block())

        @block.sync
        def _(sp):
            p.credits(sp)
            with sp.Fori(0, NT) as t:
                p.sp(sp, t)
            p.sp_end(sp)

        @block.vector
        def _(dve):
            with dve.Fori(0, NT) as t:
                p.dve(dve, t)

        @block.scalar
        def _(act):
            with act.Fori(0, NT) as t:
                p.act(act, t)

        @block.tensor
        def _(pe):
            with pe.Fori(0, NT) as t:
                p.pe(pe, t)


def norm(nc, c, y, stats, mv, var_ready, sd, sd_ready, count, rs, out):
    v = nc.vector
    c.link(v.bn_stats(stats, y))
    c.eng.nop(nofuse=True)
    v.bn_aggr(mv, stats).then_inc(var_ready, 1)
    c.eng.wait_ge(sd_ready, count)
    c.link(v.reciprocal(rs, sd))
    return v.tensor_scalar(out, y, mv[:, 0:1], rs, op0=ALU.subtract, op1=ALU.mult)


def gru_tile(nc, m, d, s):
    v, te, ac = nc.vector, nc.tensor, nc.scalar
    b4, b5, b6, b7 = s.bank
    tb = s.sb("tb", [P, NTAB, W1])
    rev = s.sb("rev", [P, W1])
    ws, safe, inv = s.sb("ws", [P, 2]), s.sb("safe", [P, 2]), s.sb("inv", [P, 2])
    nb, nbT = s.sb("nb", [P, 3 * D]), s.sb("nbT", [P, 3 * P])
    rz, u, nn, y = s.sb("rz", [P, 2 * D]), s.sb("u", [P, D]), s.sb("nn", [P, D]), s.sb("y", [P, D])
    stats, mv, sd, rs = s.sb("stats", [P, 6]), s.sb("mv", [P, 2]), s.sb("sd", [P, 1]), s.sb("rs", [P, 1])
    xs, xT, tout = s.sb("xs", [P, D]), s.sb("xT", [P, P]), s.sb("tout", [P, R * D])
    tab_in, tab_used, nb_ready, nbT_ps, nbT_ready = (s.sem("tab_in"), s.sem("tab_used"), s.sem("nb_ready"),
                                                     s.sem("nbT_ps"), s.sem("nbT_ready"))
    gates, rz_ready, pre_ready, tanh_ready = s.sem("gates"), s.sem("rz_ready"), s.sem("pre_ready"), s.sem("tanh_ready")
    var_ready, sd_ready, x_ready, xT_ps, xT_ready = (s.sem("var_ready"), s.sem("sd_ready"), s.sem("x_ready"),
                                                     s.sem("xT_ps"), s.sem("xT_ready"))
    prod, ev_act, ev_dve, written = s.sem("prod"), s.sem("ev_act"), s.sem("ev_dve"), s.sem("written")
    ident = m.consts[:, C_ID:C_ID + P]
    ident_ones = m.ones[0:1, 0:P]

    def credits(sp):
        sp.sem_inc(tab_used, 1)
        sp.sem_inc(ev_act, 2)
        sp.sem_inc(ev_dve, 3)
        sp.sem_inc(written, 16)

    def sp(sp, t):
        sp.wait_ge(tab_used, t + 1)
        sp.nop(nofuse=True)
        sp.dma_start(tb[:], d["tables"].rearrange("(k n) f -> n k f", k=NTAB)[ds(t * P, P), :, :]).then_inc(tab_in, 16)
        sp.wait_ge(ev_act, (t + 2) * 2)
        sp.nop(nofuse=True)
        sp.wait_ge(ev_dve, (t + 2) * 3)
        sp.nop(nofuse=True)
        sp.dma_start(d["rel_table"].rearrange("(n r) o -> n (r o)", r=R)[ds(t * P, P), :], tout[:]).then_inc(written, 16)

    def sp_end(sp):
        sp.wait_ge(written, 16 * (NT + 1))

    def dve(dve, t):
        c = Chain(dve, s.chain, t, s.steps)
        x, acc = tile_of(m.x, t), tile_of(m.acc, t)
        dve.wait_ge(tab_in, (t + 1) * 16)
        v.tensor_reduce(rev[:], tb[:].rearrange("p k f -> p f k"), AX.X, ALU.add).then_inc(tab_used, 1)
        dve.wait_ge(tab_used, t + 2)
        c.link(v.tensor_scalar_mul(ws[:, 0:1], m.acc[:, ds(t, 1), D:W1].rearrange("p a f -> p (a f)"), 1.0))
        c.link(v.tensor_copy(ws[:, 1:2], rev[:, D:W1]))
        c.link(v.scalar_tensor_tensor(safe[:], ws[:], 0.0, ws[:], ALU.is_le, ALU.add))
        c.link(v.reciprocal(safe[:], safe[:]))
        c.link(v.scalar_tensor_tensor(inv[:], ws[:], 0.0, safe[:], ALU.is_gt, ALU.mult))
        v.tensor_scalar_mul(nb[:, 2 * D:3 * D], x, 1.0).then_inc(nb_ready, 1)
        v.tensor_scalar(nb[:, 0:D], acc, inv[:, 0:1], None, op0=ALU.mult).then_inc(nb_ready, 1)
        v.tensor_scalar(nb[:, D:2 * D], rev[:, 0:D], inv[:, 1:2], None, op0=ALU.mult).then_inc(nb_ready, 1)
        dve.wait_ge(rz_ready, t + 1)
        c.link(v.tensor_tensor(u[:], rz[:, 0:D], b6[:, D:2 * D], ALU.mult))
        v.tensor_tensor(u[:], u[:], b6[:, 0:D], ALU.add).then_inc(pre_ready, 1)
        dve.wait_ge(tanh_ready, t + 1)
        c.link(v.tensor_tensor(y[:], x, nn[:], ALU.subtract))
        c.link(v.tensor_tensor(y[:], y[:], rz[:, D:2 * D], ALU.mult))
        c.link(v.tensor_tensor(y[:], y[:], nn[:], ALU.add))
        c.link(v.tensor_tensor(y[:], y[:], x, ALU.add))
        norm(nc, c, y[:], stats[:], mv[:], var_ready, sd[:], sd_ready, t + 1, rs[:], xs[:]).then_inc(x_ready, 1)
        dve.wait_ge(x_ready, t + 1)
        v.tensor_scalar_mul(x, xs[:], 1.0)
        dve.wait_ge(prod, t * 5 + 1)
        v.tensor_scalar_mul(acc, b6[:, 2 * D:3 * D], 1.0).then_inc(ev_dve, 1)
        v.tensor_scalar_mul(m.acc[:, ds(t, 1), D:W1].rearrange("p a f -> p (a f)"), m.zeros[:, 0:1], 1.0)
        dve.wait_ge(written, (t + 1) * 16)
        dve.wait_ge(prod, t * 5 + 3)
        v.tensor_copy(tout[:, 512:1024], b7[:]).then_inc(ev_dve, 1)
        dve.wait_ge(prod, t * 5 + 5)
        v.tensor_copy(tout[:, 1536:2048], b5[:]).then_inc(ev_dve, 1)
        c.end()

    def act(act, t):
        act.wait_ge(nbT_ps, t + 1)
        ac.activation(nbT[:], b4[:, 0:3 * P], ACT.Copy).then_inc(nbT_ready, 1)
        act.wait_ge(gates, t + 1)
        ac.activation(rz[:], b5[:, 0:2 * D], ACT.Sigmoid).then_inc(rz_ready, 1)
        act.wait_ge(pre_ready, t + 1)
        ac.activation(nn[:], u[:], ACT.Tanh).then_inc(tanh_ready, 1)
        act.wait_ge(var_ready, t + 1)
        ac.activation(sd[:], mv[:, 1:2], ACT.Sqrt, bias=m.eps[:]).then_inc(sd_ready, 1)
        act.wait_ge(xT_ps, t + 1)
        ac.activation(xT[:], b4[:, 0:P], ACT.Copy).then_inc(xT_ready, 1)
        act.wait_ge(written, (t + 1) * 16)
        act.wait_ge(prod, t * 5 + 2)
        ac.activation(tout[:, 0:512], b5[:], ACT.Copy).then_inc(ev_act, 1)
        act.wait_ge(prod, t * 5 + 4)
        ac.activation(tout[:, 1024:1536], b4[:], ACT.Copy).then_inc(ev_act, 1)

    def pe(pe, t):
        pe.wait_ge(nb_ready, (t + 1) * 3)
        pe.wait_ge(ev_act, (t + 1) * 2)
        pe.wait_ge(ev_dve, (t + 1) * 3)
        te.transpose(b4[:, 0:P], nb[:, 0:D], ident)
        te.transpose(b4[:, P:2 * P], nb[:, D:2 * D], ident)
        te.transpose(b4[:, 2 * P:3 * P], nb[:, 2 * D:3 * D], ident).then_inc(nbT_ps, 1)
        pe.wait_ge(nbT_ready, t + 1)
        n1, n2, xt = nbT[:, 0:P], nbT[:, P:2 * P], nbT[:, 2 * P:3 * P]
        te.matmul(b5[:, 0:2 * D], ident_ones, m.b_ih[:, 0:2 * D], start=True, stop=False)
        te.matmul(b5[:, 0:2 * D], ident_ones, m.b_hh[:, 0:2 * D], start=False, stop=False)
        te.matmul(b5[:, 0:2 * D], n1, m.fold[:, 0, 0:2 * D], start=False, stop=False)
        te.matmul(b5[:, 0:2 * D], n2, m.fold[:, 1, 0:2 * D], start=False, stop=False)
        te.matmul(b5[:, 0:2 * D], xt, m.whh[:, 0:2 * D], start=False, stop=True)
        te.matmul(b6[:, 0:D], ident_ones, m.b_ih[:, 2 * D:3 * D], start=True, stop=False)
        te.matmul(b6[:, 0:D], n1, m.fold[:, 0, 2 * D:3 * D], start=False, stop=False)
        te.matmul(b6[:, 0:D], n2, m.fold[:, 1, 2 * D:3 * D], start=False, stop=True)
        te.matmul(b6[:, D:2 * D], ident_ones, m.b_hh[:, 2 * D:3 * D], start=True, stop=False)
        te.matmul(b6[:, D:2 * D], xt, m.whh[:, 2 * D:3 * D], start=False, stop=True).then_inc(gates, 1)
        pe.wait_ge(x_ready, t + 1)
        te.transpose(b4[:, 0:P], xs[:], ident).then_inc(xT_ps, 1)
        pe.wait_ge(xT_ready, t + 1)
        te.matmul(b6[:, 2 * D:3 * D], ident_ones, m.b1[:], start=True, stop=False)
        te.matmul(b6[:, 2 * D:3 * D], xT[:], m.selfw[:], start=False, stop=True).then_inc(prod, 1)
        for i, bank in enumerate((b5, b7, b4, b5)):
            if i == 3:
                pe.wait_ge(ev_act, t * 2 + 3)
            te.matmul(bank[:], xT[:], m.rel[:, i * 512:(i + 1) * 512], start=True, stop=True).then_inc(prod, 1)

    return TileProgram(credits=credits, sp=sp, sp_end=sp_end, dve=dve, act=act, pe=pe)


def rgcn_tile(nc, m, d, s):
    v, te, ac = nc.vector, nc.tensor, nc.scalar
    b4, b5, b6, b7 = s.bank
    xs, deg = s.sb("xs", [P, D]), s.sb("deg", [P, 1])
    y, xT, out = s.sb("y", [P, D]), s.sb("xT", [P, P]), s.sb("out", [P, D])
    stats, mv, sd, rs = s.sb("stats", [P, 6]), s.sb("mv", [P, 2]), s.sb("sd", [P, 1]), s.sb("rs", [P, 1])
    var_ready, sd_ready, x_ready, xT_ps, xT_ready = (s.sem("var_ready"), s.sem("sd_ready"), s.sem("x_ready"),
                                                     s.sem("xT_ps"), s.sem("xT_ready"))
    prod, out_ready, written = s.sem("prod"), s.sem("out_ready"), s.sem("written")
    ident = m.consts[:, C_ID:C_ID + P]

    def credits(sp):
        sp.sem_inc(written, 16)

    def sp(sp, t):
        sp.wait_ge(out_ready, t + 1)
        sp.nop(nofuse=True)
        sp.dma_start(d["msg_table"][ds(t * P, P), :], out[:]).then_inc(written, 16)

    def sp_end(sp):
        sp.wait_ge(written, 16 * (NT + 1))

    def dve(dve, t):
        c = Chain(dve, s.chain, t, s.steps)
        x, acc = tile_of(m.x, t), tile_of(m.acc, t)
        c.link(v.tensor_scalar_max(deg[:], m.acc[:, ds(t, 1), D:W1].rearrange("p a f -> p (a f)"), 1.0))
        c.link(v.reciprocal(deg[:], deg[:]))
        v.tensor_scalar_mul(m.inv_deg[:, ds(t, 1)], deg[:], 1.0)
        c.link(v.scalar_tensor_tensor(y[:], acc, 0.0, x, ALU.max, ALU.add))
        c.link(v.tensor_scalar_mul(tile_of(m.acc, t, W1), m.zeros[:], 1.0))
        norm(nc, c, y[:], stats[:], mv[:], var_ready, sd[:], sd_ready, t + 1, rs[:], xs[:]).then_inc(x_ready, 1)
        dve.wait_ge(x_ready, t + 1)
        v.tensor_scalar_mul(x, xs[:], 1.0)
        c.end()

    def act(act, t):
        act.wait_ge(var_ready, t + 1)
        ac.activation(sd[:], mv[:, 1:2], ACT.Sqrt, bias=m.eps[:]).then_inc(sd_ready, 1)
        act.wait_ge(xT_ps, t + 1)
        ac.activation(xT[:], b4[:, 0:P], ACT.Copy).then_inc(xT_ready, 1)
        act.wait_ge(prod, t + 1)
        act.wait_ge(written, (t + 1) * 16)
        ac.activation(out[:], b5[:, 0:D], ACT.Copy).then_inc(out_ready, 1)

    def pe(pe, t):
        pe.wait_ge(x_ready, t + 1)
        te.transpose(b4[:, 0:P], xs[:], ident).then_inc(xT_ps, 1)
        pe.wait_ge(xT_ready, t + 1)
        te.matmul(b5[:, 0:D], m.ones[0:1, 0:P], m.b_msg[:], start=True, stop=False)
        te.matmul(b5[:, 0:D], xT[:], m.wmsg[:, 0, :], start=False, stop=True).then_inc(prod, 1)

    return TileProgram(credits=credits, sp=sp, sp_end=sp_end, dve=dve, act=act, pe=pe)


def mlp_tile(nc, m, d, s):
    v, te, ac = nc.vector, nc.tensor, nc.scalar
    b4, b5, b6, b7 = s.bank
    xs = s.sb("xs", [P, D])
    y, mx, mxT = s.sb("y", [P, D]), s.sb("mx", [P, 2 * D]), s.sb("mxT", [P, 2 * P])
    stats, mv, sd, rs = s.sb("stats", [P, 6]), s.sb("mv", [P, 2]), s.sb("sd", [P, 1]), s.sb("rs", [P, 1])
    var_ready, sd_ready, x_ready, mean_ready, mxT_ps, mxT_ready = (
        s.sem("var_ready"), s.sem("sd_ready"), s.sem("x_ready"), s.sem("mean_ready"), s.sem("mxT_ps"), s.sem("mxT_ready"))
    prod, written = s.sem("prod"), s.sem("written")
    ident = m.consts[:, C_ID:C_ID + P]

    def credits(sp):
        sp.sem_inc(written, 16)

    def sp(sp, t):
        sp.wait_ge(x_ready, t + 1)
        sp.nop(nofuse=True)
        sp.dma_start(d["x3_table"][ds(t * P, P), :], xs[:]).then_inc(written, 16)

    def sp_end(sp):
        sp.wait_ge(written, 16 * (NT + 1))

    def dve(dve, t):
        c = Chain(dve, s.chain, t, s.steps)
        x, acc = tile_of(m.x, t), tile_of(m.acc, t)
        v.tensor_scalar_mul(mx[:, D:2 * D], x, 1.0).then_inc(mean_ready, 1)
        v.tensor_scalar(mx[:, 0:D], acc, m.inv_deg[:, ds(t, 1)], None, op0=ALU.mult).then_inc(mean_ready, 1)
        dve.wait_ge(mean_ready, (t + 1) * 2)
        c.link(v.tensor_scalar_mul(tile_of(m.acc, t, W1), m.zeros[:], 1.0))
        dve.wait_ge(prod, t + 1)
        c.link(norm(nc, c, b5[:, 0:D], stats[:], mv[:], var_ready, sd[:], sd_ready, t * 2 + 1, rs[:], y[:]))
        c.link(v.tensor_tensor(y[:], y[:], m.gamma[:], ALU.mult))
        c.link(v.tensor_tensor(y[:], y[:], m.beta[:], ALU.add))
        c.link(v.tensor_tensor(y[:], y[:], x, ALU.add))
        c.link(v.scalar_tensor_tensor(y[:], y[:], 0.0, x, ALU.max, ALU.add))
        dve.wait_ge(written, (t + 1) * 16)
        norm(nc, c, y[:], stats[:], mv[:], var_ready, sd[:], sd_ready, t * 2 + 2, rs[:], xs[:]).then_inc(x_ready, 1)
        dve.wait_ge(x_ready, t + 1)
        v.tensor_scalar_mul(x, xs[:], 1.0)
        c.end()

    def act(act, t):
        act.wait_ge(mxT_ps, t + 1)
        ac.activation(mxT[:], b4[:, 0:2 * P], ACT.Copy).then_inc(mxT_ready, 1)
        for i in range(2):
            act.wait_ge(var_ready, t * 2 + i + 1)
            ac.activation(sd[:], mv[:, 1:2], ACT.Sqrt, bias=m.eps[:]).then_inc(sd_ready, 1)

    def pe(pe, t):
        pe.wait_ge(mean_ready, (t + 1) * 2)
        te.transpose(b4[:, 0:P], mx[:, 0:D], ident)
        te.transpose(b4[:, P:2 * P], mx[:, D:2 * D], ident).then_inc(mxT_ps, 1)
        pe.wait_ge(mxT_ready, t + 1)
        te.matmul(b5[:, 0:D], m.ones[0:1, 0:P], m.b_upd[:], start=True, stop=False)
        te.matmul(b5[:, 0:D], mxT[:, P:2 * P], m.wupd[:, 0, :], start=False, stop=False)
        te.matmul(b5[:, 0:D], mxT[:, 0:P], m.wupd[:, 1, :], start=False, stop=True).then_inc(prod, 1)

    return TileProgram(credits=credits, sp=sp, sp_end=sp_end, dve=dve, act=act, pe=pe)


def sage1_tile(nc, m, d, s):
    v, te, ac = nc.vector, nc.tensor, nc.scalar
    b4, b5, b6, b7 = s.bank
    mx, mxT, h, hT = s.sb("mx", [P, 2 * D]), s.sb("mxT", [P, 2 * P]), s.sb("h", [P, D]), s.sb("hT", [P, P])
    mean_ready, mxT_ps, mxT_ready, prod, h_ready, hT_ps, hT_ready, own, x_ready, written = (
        s.sem("mean_ready"), s.sem("mxT_ps"), s.sem("mxT_ready"), s.sem("prod"), s.sem("h_ready"), s.sem("hT_ps"),
        s.sem("hT_ready"), s.sem("own"), s.sem("x_ready"), s.sem("written"))
    ident = m.consts[:, C_ID:C_ID + P]

    def credits(sp):
        sp.sem_inc(written, 16)

    def sp(sp, t):
        sp.wait_ge(h_ready, t + 1)
        sp.nop(nofuse=True)
        sp.dma_start(d["h_table"][ds(t * P, P), :], h[:]).then_inc(written, 16)

    def sp_end(sp):
        sp.wait_ge(written, 16 * (NT + 1))

    def dve(dve, t):
        c = Chain(dve, s.chain, t, s.steps)
        x, acc = tile_of(m.x, t), tile_of(m.acc, t)
        v.tensor_scalar_mul(mx[:, D:2 * D], x, 1.0).then_inc(mean_ready, 1)
        v.tensor_scalar(mx[:, 0:D], acc, m.inv_deg[:, ds(t, 1)], None, op0=ALU.mult).then_inc(mean_ready, 1)
        dve.wait_ge(mean_ready, (t + 1) * 2)
        c.link(v.tensor_scalar_mul(tile_of(m.acc, t, W1), m.zeros[:], 1.0))
        dve.wait_ge(own, t + 1)
        v.tensor_tensor(x, x, b7[:, 0:D], ALU.add).then_inc(x_ready, 1)
        c.end()

    def act(act, t):
        act.wait_ge(mxT_ps, t + 1)
        ac.activation(mxT[:], b4[:, 0:2 * P], ACT.Copy).then_inc(mxT_ready, 1)
        act.wait_ge(prod, t + 1)
        act.wait_ge(written, (t + 1) * 16)
        ac.activation(h[:], b5[:, 0:D], ACT.Relu).then_inc(h_ready, 1)
        act.wait_ge(hT_ps, t + 1)
        ac.activation(hT[:], b6[:, 0:P], ACT.Copy).then_inc(hT_ready, 1)

    def pe(pe, t):
        pe.wait_ge(mean_ready, (t + 1) * 2)
        te.transpose(b4[:, 0:P], mx[:, 0:D], ident)
        te.transpose(b4[:, P:2 * P], mx[:, D:2 * D], ident).then_inc(mxT_ps, 1)
        pe.wait_ge(mxT_ready, t + 1)
        te.matmul(b5[:, 0:D], m.ones[0:1, 0:P], m.b31[:], start=True, stop=False)
        te.matmul(b5[:, 0:D], mxT[:, 0:P], m.wl1[:], start=False, stop=False)
        te.matmul(b5[:, 0:D], mxT[:, P:2 * P], m.wr1[:], start=False, stop=True).then_inc(prod, 1)
        pe.wait_ge(h_ready, t + 1)
        te.transpose(b6[:, 0:P], h[:], ident).then_inc(hT_ps, 1)
        pe.wait_ge(hT_ready, t + 1)
        te.matmul(b7[:, 0:D], m.ones[0:1, 0:P], m.b32[:], start=True, stop=False)
        te.matmul(b7[:, 0:D], hT[:], m.wr2[:], start=False, stop=True).then_inc(own, 1)

    return TileProgram(credits=credits, sp=sp, sp_end=sp_end, dve=dve, act=act, pe=pe)


def sage2_tile(nc, m, d, s):
    v, te, ac = nc.vector, nc.tensor, nc.scalar
    b4, b5, b6, b7 = s.bank
    y, mean, mT, out = s.sb("y", [P, D]), s.sb("mean", [P, D]), s.sb("mT", [P, P]), s.sb("out", [P, D])
    stats, mv, sd, rs = s.sb("stats", [P, 6]), s.sb("mv", [P, 2]), s.sb("sd", [P, 1]), s.sb("rs", [P, 1])
    var_ready, sd_ready, out_ready, mean_ready, mT_ps, mT_ready = (
        s.sem("var_ready"), s.sem("sd_ready"), s.sem("out_ready"), s.sem("mean_ready"), s.sem("mT_ps"), s.sem("mT_ready"))
    prod, written = s.sem("prod"), s.sem("written")
    ident = m.consts[:, C_ID:C_ID + P]

    def credits(sp):
        sp.sem_inc(written, 16)

    def sp(sp, t):
        sp.wait_ge(out_ready, t + 1)
        sp.nop(nofuse=True)
        sp.dma_start(d["out"][ds(t * P, P), :], out[:]).then_inc(written, 16)

    def sp_end(sp):
        sp.wait_ge(written, 16 * (NT + 1))

    def dve(dve, t):
        c = Chain(dve, s.chain, t, s.steps)
        x, acc = tile_of(m.x, t), tile_of(m.acc, t)
        v.tensor_scalar(mean[:], acc, m.inv_deg[:, ds(t, 1)], None, op0=ALU.mult).then_inc(mean_ready, 1)
        dve.wait_ge(prod, t + 1)
        c.link(v.tensor_tensor(y[:], x, b5[:, 0:D], ALU.add))
        dve.wait_ge(written, (t + 1) * 16)
        norm(nc, c, y[:], stats[:], mv[:], var_ready, sd[:], sd_ready, t + 1, rs[:], out[:]).then_inc(out_ready, 1)
        c.end()

    def act(act, t):
        act.wait_ge(mT_ps, t + 1)
        ac.activation(mT[:], b4[:, 0:P], ACT.Copy).then_inc(mT_ready, 1)
        act.wait_ge(var_ready, t + 1)
        ac.activation(sd[:], mv[:, 1:2], ACT.Sqrt, bias=m.eps[:]).then_inc(sd_ready, 1)

    def pe(pe, t):
        pe.wait_ge(mean_ready, t + 1)
        te.transpose(b4[:, 0:P], mean[:], ident).then_inc(mT_ps, 1)
        pe.wait_ge(mT_ready, t + 1)
        te.matmul(b5[:, 0:D], mT[:], m.wl2[:], start=True, stop=True).then_inc(prod, 1)

    return TileProgram(credits=credits, sp=sp, sp_end=sp_end, dve=dve, act=act, pe=pe)



def program(nc, d):
    with ExitStack() as ctx:
        def sb(name, shape, dt=F32):
            return ctx.enter_context(nc.sbuf_tensor(name, shape, dt))

        m = Memory()
        m.x = sb("x", [P, NT, W1])
        m.items = sb("items", [P, 4, ITEMS])
        m.item_tc = sb("item_tc", [1, 2 * ITEMS], I32)
        m.inv_deg = sb("inv_deg", [P, NT])
        m.consts = sb("consts", [P, C_W])
        m.ones = sb("ones", [1, P])
        m.zeros = sb("zeros", [P, W1])
        m.eps = sb("eps", [P, 1])
        m.fold = sb("fold", [P, 2, 3 * D])
        m.whh = sb("whh", [P, 3 * D])
        m.b_ih, m.b_hh = sb("b_ih", [1, 3 * D]), sb("b_hh", [1, 3 * D])
        m.rel = sb("rel", [P, R * D])
        m.selfw, m.b1 = sb("selfw", [P, D]), sb("b1", [1, D])
        m.wmsg, m.b_msg = sb("wmsg", [P, 2, D]), sb("b_msg", [1, D])
        m.wupd, m.b_upd = sb("wupd", [P, 2, D]), sb("b_upd", [1, D])
        m.gamma, m.beta = sb("gamma", [P, D]), sb("beta", [P, D])
        m.wl1, m.wr1, m.b31 = sb("wl1", [P, D]), sb("wr1", [P, D]), sb("b31", [1, D])
        m.wl2, m.wr2, m.b32 = sb("wl2", [P, D]), sb("wr2", [P, D]), sb("b32", [1, D])

        plan_phase(nc, m, d)
        m.acc = sb("acc", [P, NT, W1])
        scatter_phase(nc, m, d)
        gather_phase(nc, m, d, "fwd", d["x_pad"], 0, True, False)
        tile_phase(nc, m, d, "gru", 12, gru_tile)
        gather_phase(nc, m, d, "rel", d["rel_table"], 3, False, False)
        tile_phase(nc, m, d, "rgcn", 6, rgcn_tile)
        gather_phase(nc, m, d, "mlp", d["msg_table"], 0, False, True)
        tile_phase(nc, m, d, "upd", 10, mlp_tile)
        gather_phase(nc, m, d, "hop1", d["x3_table"], 0, False, False)
        tile_phase(nc, m, d, "sage1", 1, sage1_tile)
        gather_phase(nc, m, d, "hop2", d["h_table"], 0, False, False)
        tile_phase(nc, m, d, "sage2", 3, sage2_tile)


def kernel(**inputs):
    import concourse.bacc as bacc
    from concourse.bass_utils import run_bass_kernel_spmd as run

    a = {k: np.asarray(v) for k, v in inputs.items()}
    slots = (NC + 1) * P

    def padded(v, n, fill):
        out = np.full((n,) + v.shape[1:], fill, v.dtype)
        out[:v.shape[0]] = v
        return out

    src = padded(a["src"], slots, 0).reshape(NC + 1, P)
    dst = padded(a["dst"], slots, NO_NODE).reshape(NC + 1, P)
    typ = padded(a["edge_type_16"], slots, 0).reshape(NC + 1, P)
    arrays = {
        "x_pad": padded(a["x"], NPAD, 0),
        "first_dst": dst[:, 0].reshape(1, NC + 1),
        "dst_rows": dst,
        "edge_rows": np.concatenate([src, dst, typ], axis=1),
        "weight_rows": padded(a["edge_weight"], slots, 0).reshape(NC + 1, P),
        "attr_t": padded(a["edge_attr_128"], slots, 0).reshape(NC + 1, P, D).transpose(0, 2, 1),
        "consts": constants(),
        "L0_gnn_W1": a["L0_gnn_W1"], "L0_gnn_W2": a["L0_gnn_W2"],
        "w_ih_t": a["L0_gnn_w_ih"].T, "w_hh_t": a["L0_gnn_w_hh"].T,
        "b_ih": a["L0_gnn_b_ih"][None], "b_hh": a["L0_gnn_b_hh"][None],
        "rel_t": a["L1_gnn_relation_weights"].transpose(1, 0, 2).reshape(D, R * D),
        "L1_gnn_self_weight": a["L1_gnn_self_weight"], "L1_bias": a["L1_gnn_bias"][None],
        "L2_gnn_W_msg": a["L2_gnn_W_msg"], "b_msg": a["L2_gnn_b_msg"][None],
        "L2_gnn_W_upd": a["L2_gnn_W_upd"], "b_upd": a["L2_gnn_b_upd"][None],
        "gamma": a["L2_gnn_gamma"][None], "beta": a["L2_gnn_beta"][None],
        "wl1_t": a["L3_gnn_Wl1"].T, "wr1_t": a["L3_gnn_Wr1"].T, "b31": a["L3_gnn_b1"][None],
        "wl2_t": a["L3_gnn_Wl2"].T, "wr2_t": a["L3_gnn_Wr2"].T, "b32": a["L3_gnn_b2"][None],
    }
    arrays = {k: np.ascontiguousarray(v) for k, v in arrays.items()}
    nc = bacc.Bacc("TRN2", target_bir_lowering=False, num_devices=1)
    aps = {k: nc.dram_tensor(f"in_{k}", v.shape, mybir.dt.from_np(v.dtype), kind="ExternalInput").ap() for k, v in arrays.items()}
    d = dict(aps)
    d["out"] = nc.dram_tensor("out", (NPAD, D), F32, kind="ExternalOutput").ap()
    d["tables"] = nc.dram_tensor("tables", (NTAB * TROWS, W1), F32).ap()
    d["rel_table"] = nc.dram_tensor("rel_table", (NPAD * R, D), F32).ap()
    d["msg_table"] = nc.dram_tensor("msg_table", (NPAD, D), F32).ap()
    d["x3_table"] = nc.dram_tensor("x3_table", (NPAD, D), F32).ap()
    d["h_table"] = nc.dram_tensor("h_table", (NPAD, D), F32).ap()
    d["tc_dram"] = nc.dram_tensor("tc_dram", (2 * JC, P), I32).ap()
    program(nc, d)
    r = run(nc, [{f"in_{k}": v for k, v in arrays.items()}], core_ids=[0])
    return r.results[0]["out"][:N]
```

```python
from contextlib import ExitStack

import numpy as np

import concourse.bass as bass
from concourse import mybir

F32 = mybir.dt.float32
I32 = mybir.dt.int32
ALU = mybir.AluOpType
ACT = mybir.ActivationFunctionType
AX = mybir.AxisListType
ds = bass.ds


class Memory:
    pass


class Step:
    pass


class TileProgram:

    def __init__(self, credits, sp, sp_end, dve, act, pe):
        self.credits, self.sp, self.sp_end, self.dve, self.act, self.pe = credits, sp, sp_end, dve, act, pe


P = 128
N = 12500
E = 200000
D = 128
R = 16
NT = -(-N // P)
NPAD = NT * P
NC = -(-E // P)
SLOTS = 16
QUAD = 4
NQ = SLOTS // QUAD
GROUPS = -(-(NC + NT - 1) // SLOTS)
ITEMS = GROUPS * SLOTS
JC = ITEMS // P
W1 = D + 1
NTAB = 8
TRASH = NPAD
TROWS = NPAD + P
NO_NODE = 1 << 20
EPS = 1e-5
assert ITEMS % P == 0 and JC * P == ITEMS

C_ID, C_IOTA, C_LOW, C_K, C_TRASH, C_BOUND = 0, P, 2 * P, 3 * P, 3 * P + JC, 3 * P + JC + 1
C_TAB = C_BOUND + 1
C_W = C_TAB + NTAB


def constants():
    c = np.zeros((P, C_W), np.float32)
    c[:, C_ID:C_ID + P] = np.eye(P)
    c[:, C_IOTA:C_IOTA + P] = np.arange(P)[None, :]
    c[:, C_LOW:C_LOW + P] = np.tril(np.ones((P, P)), -1)
    c[:, C_K:C_K + JC] = np.arange(JC)[None, :] * P + np.arange(P)[:, None]
    c[:, C_TRASH] = TRASH + np.arange(P)
    c[:, C_BOUND] = P * np.arange(P)
    c[:, C_TAB:C_TAB + NTAB] = TROWS * np.arange(NTAB)[None, :]
    return c


def column(ap, n):
    return ap.to_broadcast([P, n])



def plan_phase(nc, m, d):
    with ExitStack() as ctx:
        def sb(name, shape, dt=F32):
            return ctx.enter_context(nc.sbuf_tensor(name, shape, dt))

        def ps(name):
            return ctx.enter_context(nc.psum_tensor(name, [P, 512], F32))

        def sem(name):
            return ctx.enter_context(nc.semaphore(name))

        firsts_i = sb("firsts_i", [P, NC + 1], I32)
        firsts = sb("firsts", [P, NC + 1])
        below = sb("below", [P, NC + 1])
        nfirst = sb("nfirst", [P, 1])
        lastrow = sb("lastrow", [P, 1])
        lastrow_i = sb("lastrow_i", [P, 1], I32)
        drow_i = sb("drow_i", [P, P], I32)
        drow = sb("drow", [P, P])
        inrow = sb("inrow", [P, 1])
        start_col = sb("start_col", [P, 1])
        start = sb("start", [P, P])
        lo_i = sb("lo_i", [P, NT], I32)
        lo_s = sb("lo_s", [P, NT], I32)
        lo = sb("lo", [P, NT])
        hi_f = sb("hi_f", [P, NT])
        hi_i = sb("hi_i", [P, NT], I32)
        hi_s = sb("hi_s", [P, NT], I32)
        hi = sb("hi", [P, NT])
        some = sb("some", [P, NT])
        cnt = sb("cnt", [P, NT])
        one = sb("one", [P, NT])
        incl = sb("incl", [P, NT])
        first = sb("first", [P, NT])
        g = sb("g", [P, NT])
        dg = sb("dg", [P, NT])
        mask = sb("mask", [P, 2, NT])
        ntile = sb("ntile", [P, JC])
        goff = sb("goff", [P, JC])
        valid = sb("valid", [P, JC])
        chunk = sb("chunk", [P, JC])
        tile = sb("tile", [P, JC])
        base = sb("base", [P, JC])
        chunk_i = sb("chunk_i", [P, JC], I32)
        rows_i = sb("rows_i", [P, JC, 3 * P], I32)
        rows_w = sb("rows_w", [P, JC, P])
        rows = sb("rows", [P, 4, JC, P])
        tc_i = sb("tc_i", [2 * JC, P], I32)
        w1 = sb("w1", [P, P])
        w2 = sb("w2", [P, P])
        wih = sb("wih", [P, 2, 3 * D])
        pa, pb, pc, pd = ps("pa"), ps("pb"), ps("pc"), ps("pd")

        load_firsts, load_const, load_x, load_w = sem("load_firsts"), sem("load_const"), sem("load_x"), sem("load_w")
        chain, act_chain = sem("plan_chain"), sem("act_chain")
        row_idx, row_in, start_ps, start_sb = sem("row_idx"), sem("row_in"), sem("start_ps"), sem("start_sb")
        chunk_ready, rows_in, rows_ready, rows_tp, rows_done = (sem("chunk_ready"), sem("rows_in"), sem("rows_ready"),
                                                                 sem("rows_tp"), sem("rows_done"))
        tc_ready, tc_ps, tc_sb, tc_dram, tc_row = sem("tc_ready"), sem("tc_ps"), sem("tc_sb"), sem("tc_dram"), sem("tc_row")
        fold_ps, fold_sb = sem("fold_ps"), sem("fold_sb")
        tcol = sb("tcol", [P, 2, JC])
        groups_f, groups_i = sb("groups_f", [1, NT]), sb("groups_i", [1, NT], I32)
        consts = m.consts
        block = ctx.enter_context(nc.Block())

        @block.sync
        def _(sp):
            sp.dma_start(firsts_i[:], d["first_dst"].partition_broadcast(P)).then_inc(load_firsts, 16)
            sp.dma_start(consts[:], d["consts"]).then_inc(load_const, 16)
            sp.dma_start(w1[:], d["L0_gnn_W1"]).then_inc(load_w, 16)
            sp.dma_start(w2[:], d["L0_gnn_W2"]).then_inc(load_w, 16)
            sp.dma_start(wih[:], d["w_ih_t"].rearrange("(h p) g -> p h g", h=2)).then_inc(load_w, 16)
            sp.dma_start(m.x[:, :, 0:D], d["x_pad"].rearrange("(t p) f -> p t f", p=P)).then_inc(load_x, 16)
            loads = [(m.whh[:], d["w_hh_t"]), (m.b_ih[:], d["b_ih"]), (m.b_hh[:], d["b_hh"]), (m.rel[:], d["rel_t"]),
                     (m.selfw[:], d["L1_gnn_self_weight"]), (m.b1[:], d["L1_bias"]),
                     (m.wmsg[:], d["L2_gnn_W_msg"].rearrange("(h p) o -> p h o", h=2)), (m.b_msg[:], d["b_msg"]),
                     (m.wupd[:], d["L2_gnn_W_upd"].rearrange("(h p) o -> p h o", h=2)), (m.b_upd[:], d["b_upd"]),
                     (m.gamma[:], d["gamma"].partition_broadcast(P)), (m.beta[:], d["beta"].partition_broadcast(P)),
                     (m.wl1[:], d["wl1_t"]), (m.wr1[:], d["wr1_t"]), (m.b31[:], d["b31"]),
                     (m.wl2[:], d["wl2_t"]), (m.wr2[:], d["wr2_t"]), (m.b32[:], d["b32"])]
            for to, src in loads:
                sp.dma_start(to, src).then_inc(load_x, 16)
            sp.wait_ge(tc_sb, 1)
            sp.dma_start(d["tc_dram"], tc_i[:]).then_inc(tc_dram, 16)
            sp.wait_ge(tc_dram, 16)
            sp.dma_start(m.item_tc[:], d["tc_dram"].rearrange("(a b) p -> a (b p)", a=1)).then_inc(tc_row, 16)
            sp.wait_ge(tc_row, 16)
            sp.wait_ge(load_x, 16 * (1 + len(loads)))

        @block.gpsimd
        def _(pool):
            pool.memset(m.ones[:], 1.0)
            pool.memset(m.zeros[:], 0.0)
            pool.memset(m.items[:, :, ITEMS:ITEMS + SLOTS], 0.0)
            pool.memset(m.eps[:], EPS)
            pool.memset(m.x[:, :, D:W1], 1.0)
            pool.wait_ge(row_idx, 1)
            pool.indirect_dma_start(out=drow_i[:], out_offset=None, in_=d["dst_rows"],
                                    in_offset=bass.IndirectOffsetOnAxis(ap=lastrow_i[:], axis=0)).then_inc(row_in, 16)
            pool.wait_ge(chunk_ready, 1)
            for j in range(JC):
                pool.indirect_dma_start(out=rows_i[:, j, :], out_offset=None, in_=d["edge_rows"],
                                        in_offset=bass.IndirectOffsetOnAxis(ap=chunk_i[:, j:j + 1], axis=0)).then_inc(rows_in, 16)
                pool.indirect_dma_start(out=rows_w[:, j, :], out_offset=None, in_=d["weight_rows"],
                                        in_offset=bass.IndirectOffsetOnAxis(ap=chunk_i[:, j:j + 1], axis=0)).then_inc(rows_in, 16)

        @block.vector
        def _(dve):
            n = [0]

            def link(ins):
                n[0] += 1
                ins.then_inc(chain, 1)
                dve.wait_ge(chain, n[0])

            v = nc.vector
            k = consts[:, C_K:C_K + JC]
            bound = consts[:, C_BOUND:C_BOUND + 1]
            dve.wait_ge(load_firsts, 16)
            link(v.tensor_copy(firsts[:], firsts_i[:]))
            dve.wait_ge(load_const, 16)
            link(v.tensor_scalar(below[:], firsts[:], bound, None, op0=ALU.is_lt, op1=ALU.add, accum_out=nfirst[:]))
            link(v.tensor_scalar(lastrow[:], nfirst[:], -1.0, 0.0, op0=ALU.add, op1=ALU.max))
            v.tensor_copy(lastrow_i[:], lastrow[:]).then_inc(row_idx, 1)
            dve.wait_ge(row_in, 16)
            link(v.tensor_copy(drow[:], drow_i[:]))
            link(v.tensor_scalar(below[:, 0:P], drow[:], bound, None, op0=ALU.is_lt, op1=ALU.add, accum_out=inrow[:]))
            v.scalar_tensor_tensor(start_col[:], lastrow[:], float(P), inrow[:], ALU.mult, ALU.add).then_inc(start_sb, 1)
            dve.wait_ge(start_ps, 1)
            link(v.tensor_copy(start[:], pa[:, 0:P]))
            link(v.tensor_copy(lo_i[:], start[:, 0:NT]))
            link(v.tensor_scalar(lo_s[:], lo_i[:], 7, None, op0=ALU.arith_shift_right))
            link(v.tensor_copy(lo[:], lo_s[:]))
            link(v.tensor_scalar_add(hi_f[:], start[:, 1:NT + 1], float(P - 1)))
            link(v.tensor_copy(hi_i[:], hi_f[:]))
            link(v.tensor_scalar(hi_s[:], hi_i[:], 7, None, op0=ALU.arith_shift_right))
            link(v.tensor_copy(hi[:], hi_s[:]))
            link(v.tensor_tensor(some[:], start[:, 1:NT + 1], start[:, 0:NT], ALU.is_gt))
            link(v.tensor_tensor(cnt[:], hi[:], lo[:], ALU.subtract))
            link(v.tensor_tensor(cnt[:], cnt[:], some[:], ALU.mult))
            link(v.memset(one[:], 1.0))
            link(v.tensor_tensor_scan(incl[:], one[:], cnt[:], 0.0, ALU.mult, ALU.add))
            link(v.tensor_tensor(first[:], incl[:], cnt[:], ALU.subtract))
            link(v.tensor_scalar_add(groups_f[:], incl[0:1, :], float(SLOTS - 1)))
            link(v.tensor_copy(groups_i[:], groups_f[:]))
            link(v.memset(m.tile_steps[:], 0))
            link(v.tensor_scalar(m.tile_steps[:, 1:NT], groups_i[:, 0:NT - 1], SLOTS.bit_length() - 1, None,
                                 op0=ALU.arith_shift_right))
            link(v.memset(m.tile_steps[:, NT:NT + 1], GROUPS))
            link(v.tensor_tensor(g[:], lo[:], first[:], ALU.subtract))
            link(v.tensor_copy(dg[:, 0:1], g[:, 0:1]))
            link(v.tensor_tensor(dg[:, 1:NT], g[:, 1:NT], g[:, 0:NT - 1], ALU.subtract))
            for j in range(JC):
                link(v.tensor_scalar(mask[:, 0, :], first[:], k[:, j:j + 1], None, op0=ALU.is_le, op1=ALU.add,
                                     accum_out=ntile[:, j:j + 1]))
                link(v.scalar_tensor_tensor(mask[:, 1, :], first[:], k[:, j:j + 1], dg[:], ALU.is_le, ALU.mult,
                                            accum_out=goff[:, j:j + 1]))
            link(v.tensor_scalar(valid[:], k, incl[:, NT - 1:NT], None, op0=ALU.is_lt))
            link(v.tensor_scalar_add(tile[:], ntile[:], -1.0))
            link(v.tensor_tensor(chunk[:], k, goff[:], ALU.add))
            link(v.scalar_tensor_tensor(chunk[:], chunk[:], -float(NC), valid[:], ALU.add, ALU.mult))
            link(v.tensor_scalar_add(chunk[:], chunk[:], float(NC)))
            v.tensor_copy(chunk_i[:], chunk[:]).then_inc(chunk_ready, 1)
            link(v.tensor_copy(tcol[:, 0, :], tile[:]))
            v.tensor_copy(tcol[:, 1, :], chunk[:]).then_inc(tc_ready, 1)
            link(v.tensor_scalar_mul(base[:], tile[:], float(P)))
            dve.wait_ge(tc_ps, 1)
            v.tensor_copy(tc_i[:], pb[0:2 * JC, 0:P]).then_inc(tc_sb, 1)
            dve.wait_ge(rows_in, 16 * 2 * JC)
            link(v.tensor_copy(rows[:, 0, :, :], rows_i[:, :, 0:P]))
            link(v.tensor_copy(rows[:, 1, :, :], rows_i[:, :, P:2 * P]))
            link(v.tensor_tensor(rows[:, 1, :, :], rows[:, 1, :, :],
                                 base[:].unsqueeze(2).to_broadcast([P, JC, P]), ALU.subtract))
            link(v.tensor_copy(rows[:, 2, :, :], rows_w[:]))
            link(v.tensor_copy(rows[:, 3, :, :], rows_i[:, :, 2 * P:3 * P]))
            v.scalar_tensor_tensor(rows[:, 3, :, :], rows[:, 0, :, :], float(R), rows[:, 3, :, :],
                                   ALU.mult, ALU.add).then_inc(rows_ready, 1)

        @block.tensor
        def _(pe):
            ident = consts[:, C_ID:C_ID + P]
            pe.wait_ge(load_const, 16)
            pe.wait_ge(load_w, 48)
            nc.tensor.matmul(pc[:, 0:3 * D], w1[:], wih[:, 0, :], start=True, stop=True).then_inc(fold_ps, 1)
            nc.tensor.matmul(pd[:, 0:3 * D], w2[:], wih[:, 1, :], start=True, stop=True).then_inc(fold_ps, 1)
            pe.wait_ge(start_sb, 1)
            nc.tensor.matmul(pa[:, 0:P], column(start_col[:], P), ident, start=True, stop=True).then_inc(start_ps, 1)
            pe.wait_ge(tc_ready, 1)
            nc.tensor.transpose(pb[0:2 * JC, 0:P], tcol[:].rearrange("p a j -> p (a j)"), ident).then_inc(tc_ps, 1)
            pe.wait_ge(rows_ready, 1)
            pe.wait_ge(fold_sb, 1)
            for j in range(JC):
                if j:
                    pe.wait_ge(rows_done, j)
                for a in range(4):
                    last = nc.tensor.transpose(pc[:, a * P:(a + 1) * P], rows[:, a, j, :], ident)
                last.then_inc(rows_tp, 1)

        @block.scalar
        def _(act):
            act.wait_ge(fold_ps, 2)
            nc.scalar.activation(m.fold[:, 0, :], pc[:, 0:3 * D], ACT.Copy)
            nc.scalar.activation(m.fold[:, 1, :], pd[:, 0:3 * D], ACT.Copy).then_inc(fold_sb, 1)
            with act.Fori(0, JC) as j:
                act.wait_ge(rows_tp, j + 1)
                act.nop(nofuse=True)
                nc.scalar.activation(m.items[:, :, ds(j * P, P)], pc[:].rearrange("p (a b) -> p a b", a=4),
                                     ACT.Copy).then_inc(rows_done, 1)


def load4(nc, engine, ap, top):
    return nc.values_load_multi_w_load_instructions(ap, engines=(engine,), min_val=0, max_val=top,
                                                    skip_runtime_bounds_check_because="the plan writes only tiles and chunks that there are")[1]



def scatter_phase(nc, m, d):
    with ExitStack() as ctx:
        def sb(name, shape, dt=F32):
            return ctx.enter_context(nc.sbuf_tensor(name, shape, dt))

        def ps(name, n):
            return ctx.enter_context(nc.psum_tensor(name, [P, n, 512], F32))

        def sem(name):
            return ctx.enter_context(nc.semaphore(name))

        src_row, ps_m, ps_z = ps("ps_src", 2), ps("ps_m", 2), ps("ps_z", 4)
        ohw = sb("ohw", [P, 2, QUAD, P])
        same = sb("same", [P, 2, QUAD, P])
        tmp = sb("tmp", [P, QUAD, P])
        dup = sb("dup", [P, QUAD])
        away = sb("away", [P, QUAD])
        m_sb = sb("m_sb", [P, 2, QUAD, P])
        z_sb = sb("z_sb", [P, SLOTS, W1])
        ix = sb("ix", [P, SLOTS], I32)
        src_col = sb("src_col", [P, 2, QUAD])
        to_trash = sb("to_trash", [P, ITEMS])
        row_of = sb("row_of", [P, ITEMS])
        src_ready = sem("src_ready")
        tables_zero, rows_ps, same_ready, idx_ready, m_ps, m_ready, z_ps, z_ready = (
            sem("tables_zero"), sem("rows_ps"), sem("same_ready"), sem("idx_ready"),
            sem("m_ps"), sem("m_ready"), sem("z_ps"), sem("z_ready"))
        ohw_ready, chain = sem("ohw_ready"), sem("b_chain")
        freed, away_ready = sem("freed"), sem("away_ready")
        landed = [sem(f"landed{q}") for q in range(NQ)]
        block = ctx.enter_context(nc.Block())
        K = 3

        @block.sync
        def _(sp):
            rows = TROWS // P
            zp = m.zeros[:].unsqueeze(1).to_broadcast([P, rows, W1])
            for k in range(NTAB):
                sp.dma_start(d["tables"][k * TROWS:(k + 1) * TROWS, :].rearrange("(p r) f -> p r f", p=P), zp).then_inc(tables_zero, 16)
            sp.sem_inc(m_ready, 2)
            sp.sem_inc(z_ready, 2)
            sp.sem_inc(freed, NQ)
            with sp.Fori(0, GROUPS) as j:
                for q in range(NQ):
                    sp.wait_ge(landed[q], (j + 1) * (QUAD * 16))
                    sp.nop(nofuse=True)
                    sp.sem_inc(freed, 1)

        @block.gpsimd
        def _(pool):
            pool.wait_ge(tables_zero, 16 * NTAB)
            with pool.Fori(0, GROUPS) as j:
                for q in range(NQ):
                    pool.wait_ge(freed, j * NQ + q + NQ - 1)
                    pool.wait_ge(idx_ready, j * NQ + q + 1)
                    pool.wait_ge(z_ready, j * NQ + q + 1 + 2)
                    pool.nop(nofuse=True)
                    for i in range(QUAD):
                        s = q * QUAD + i
                        pool.indirect_dma_start(
                            out=d["tables"], out_offset=bass.IndirectOffsetOnAxis(ap=ix[:, s:s + 1], axis=0),
                            in_=z_sb[:, s, :], in_offset=None, compute_op=ALU.add).then_inc(landed[q], 16)
            for q in range(NQ):
                pool.wait_ge(landed[q], GROUPS * QUAD * 16)

        @block.vector
        def _(dve):
            v = nc.vector
            iota = m.consts[:, C_IOTA:C_IOTA + P].unsqueeze(1).to_broadcast([P, QUAD, P])
            low = m.consts[:, C_LOW:C_LOW + P].unsqueeze(1).to_broadcast([P, QUAD, P])
            trash = m.consts[:, C_TRASH:C_TRASH + 1]
            tab = m.consts[:, C_TAB:C_TAB + NTAB].unsqueeze(1).to_broadcast([P, ITEMS // NTAB, NTAB])
            v.tensor_scalar(to_trash[:], m.items[:, 0, 0:ITEMS], -1.0, trash, op0=ALU.mult, op1=ALU.add).then_inc(chain, 1)
            v.tensor_tensor(row_of[:].rearrange("p (a b) -> p a b", b=NTAB),
                            m.items[:, 0, 0:ITEMS].rearrange("p (a b) -> p a b", b=NTAB), tab, ALU.add).then_inc(chain, 1)
            v.tensor_copy(src_col[:, 0, :], m.items[:, 0, 0:QUAD]).then_inc(src_ready, 1)
            dve.wait_ge(chain, 2)
            with dve.Fori(0, GROUPS) as j:
                for q in range(NQ):
                    b = q % 2
                    t = j * NQ + q

                    def link(ins, n):
                        ins.then_inc(chain, 1)
                        dve.wait_ge(chain, t * K + 2 + n)

                    k0 = j * SLOTS + q * QUAD
                    dve.wait_ge(rows_ps, t + 1)
                    v.tensor_scalar_mul(src_col[:, 1 - b, :], m.items[:, 0, ds(k0 + QUAD, QUAD)], 1.0).then_inc(src_ready, 1)
                    dve.wait_ge(m_ready, t + 1)
                    dloc = m.items[:, 1, ds(k0, QUAD)].unsqueeze(2).to_broadcast([P, QUAD, P])
                    w = m.items[:, 2, ds(k0, QUAD)].unsqueeze(2).to_broadcast([P, QUAD, P])
                    src = m.items[:, 0, ds(k0, QUAD)].unsqueeze(2).to_broadcast([P, QUAD, P])
                    v.tensor_tensor(same[:, b], src_row[:, b, :].rearrange("p (i e) -> p i e", i=QUAD), src,
                                    ALU.is_equal).then_inc(same_ready, 1)
                    link(v.tensor_tensor(ohw[:, b], iota, dloc, ALU.is_equal), 1)
                    v.tensor_tensor(ohw[:, b], ohw[:, b], w, ALU.mult).then_inc(ohw_ready, 1)
                    dve.wait_ge(same_ready, t + 1)
                    link(v.tensor_tensor(tmp[:], same[:, b], low, ALU.mult), 2)
                    v.tensor_reduce(dup[:], tmp[:], AX.X, ALU.add).then_inc(chain, 1)
                    dve.wait_ge(freed, t + 1)
                    dve.wait_ge(chain, t * K + 2 + 3)
                    v.scalar_tensor_tensor(away[:], dup[:], 0.0, to_trash[:, ds(k0, QUAD)], ALU.is_gt, ALU.mult).then_inc(away_ready, 1)
                    dve.wait_ge(away_ready, t + 1)
                    v.tensor_tensor(ix[:, q * QUAD:(q + 1) * QUAD], away[:], row_of[:, ds(k0, QUAD)], ALU.add).then_inc(idx_ready, 1)

        @block.tensor
        def _(pe):
            ident = m.consts[:, C_ID:C_ID + P]

            def src_rows(b, n):
                pe.wait_ge(src_ready, n)
                for i in range(QUAD):
                    last = nc.tensor.matmul(src_row[:, b, i * P:(i + 1) * P], column(src_col[:, b, i:i + 1], P),
                                            ident, start=True, stop=True)
                last.then_inc(rows_ps, 1)

            src_rows(0, 1)
            with pe.Fori(0, GROUPS) as j:
                for q in range(NQ):
                    b = q % 2
                    t = j * NQ + q
                    k0 = j * SLOTS + q * QUAD
                    tiles = load4(nc, mybir.EngineType.PE, m.item_tc[0:1, ds(k0, QUAD)], NT - 1)
                    pe.wait_ge(same_ready, t + 1)
                    src_rows(1 - b, t + 2)
                    pe.wait_ge(ohw_ready, t + 1)
                    for i in range(QUAD):
                        last = nc.tensor.matmul(ps_m[:, b, i * P:(i + 1) * P], ohw[:, b, i, :], same[:, b, i, :],
                                                start=True, stop=True)
                    last.then_inc(m_ps, 1)
                    pe.wait_ge(m_ready, t + 1 + 2)
                    pe.wait_ge(z_ready, t + 1)
                    for i in range(QUAD):
                        last = nc.tensor.matmul(ps_z[:, 2 * b + i // 2, (i % 2) * W1:(i % 2 + 1) * W1], m_sb[:, b, i, :],
                                                m.x[:, ds(tiles[i], 1), :].rearrange("p a f -> p (a f)"), start=True, stop=True)
                    last.then_inc(z_ps, 1)

        @block.scalar
        def _(act):
            with act.Fori(0, GROUPS) as j:
                for q in range(NQ):
                    b = q % 2
                    t = j * NQ + q
                    act.wait_ge(m_ps, t + 1)
                    nc.scalar.activation(m_sb[:, b].rearrange("p i e -> p (i e)"), ps_m[:, b, :], ACT.Copy).then_inc(m_ready, 1)
                    act.wait_ge(z_ps, t + 1)
                    act.wait_ge(freed, t + 1)
                    nc.scalar.activation(z_sb[:, q * QUAD:(q + 1) * QUAD, :].rearrange("p (h i) f -> p h (i f)", h=2),
                                         ps_z[:, 2 * b:2 * b + 2, 0:2 * W1], ACT.Copy).then_inc(z_ready, 1)



class Chain:

    def __init__(self, eng, sem, t, steps):
        self.eng, self.sem, self.base, self.steps, self.n = eng, sem, t * steps, steps, 0

    def link(self, ins):
        self.n += 1
        ins.then_inc(self.sem, 1)
        self.eng.wait_ge(self.sem, self.base + self.n)

    def end(self):
        assert self.n == self.steps, self.n


def tile_of(a, t, n=D):
    return a[:, ds(t, 1), 0:n].rearrange("p a f -> p (a f)")


def layer_phase(nc, m, d, name, table, idx_row, weighted, edge_mlp, banks, steps, body):
    with ExitStack() as ctx:
        def sb(nm, shape, dt=F32):
            return ctx.enter_context(nc.sbuf_tensor(f"{name}_{nm}", shape, dt))

        def sem(nm):
            return ctx.enter_context(nc.semaphore(f"{name}_{nm}"))

        s = Step()
        s.sb, s.sem = sb, sem
        sums = ctx.enter_context(nc.psum_tensor(f"{name}_sums", [P, 4, 512], F32))
        s.bank = [ctx.enter_context(nc.psum_tensor(f"{name}_bank{i}", [P, 512], F32)) for i in range(banks)]
        s.chain, s.steps = sem("chain"), steps
        rows = sb("rows", [P, SLOTS, W1])
        oh = sb("oh", [P, SLOTS, P])
        ix = sb("ix", [P, SLOTS], I32)
        ix_ready, oh_eq, oh_ready, summed, added, ones_ready = (
            sem("ix_ready"), sem("oh_eq"), sem("oh_ready"), sem("summed"), sem("added"), sem("ones_ready"))
        gathered = [sem(f"gathered{q}") for q in range(NQ)]
        summand = rows
        if edge_mlp:
            attr = sb("attr", [P, SLOTS, P])
            msg = summand = sb("msg", [P, SLOTS, W1])
            ps_msg = ctx.enter_context(nc.psum_tensor(f"{name}_msg_bank", [P, 2, 512], F32))
            msg_ps, msg_ready = sem("msg_ps"), sem("msg_ready")
            attr_in = [sem(f"attr_in{q}") for q in range(NQ)]
        p = body(nc, m, d, s)
        block = ctx.enter_context(nc.Block())

        def over_tiles(eng, group, tile):
            with eng.Fori(0, NT) as t:
                first = eng.value_load(m.tile_steps[0:1, ds(t, 1)], min_val=0, max_val=GROUPS)
                end = eng.value_load(m.tile_steps[0:1, ds(t + 1, 1)], min_val=0, max_val=GROUPS)
                with eng.If(first < end):
                    with eng.Fori(first, end) as j:
                        group(j)
                tile(t)

        @block.sync
        def _(sp):
            sp.sem_inc(summed, NQ)
            sp.sem_inc(added, 2 * QUAD)
            p.credits(sp)
            if edge_mlp:
                sp.sem_inc(msg_ready, 2)
                with sp.Fori(0, GROUPS) as j:
                    for q in range(NQ):
                        chunks = load4(nc, mybir.EngineType.SP, m.item_tc[0:1, ds(ITEMS + j * SLOTS + q * QUAD, QUAD)], NC)
                        sp.wait_ge(summed, j * NQ + q + 1)
                        sp.nop(nofuse=True)
                        for i in range(QUAD):
                            sp.dma_start(attr[:, q * QUAD + i, :], d["attr_t"][ds(chunks[i], 1), :, :].rearrange("c f e -> (c f) e")
                                         ).then_inc(attr_in[q], 16)
            else:
                with sp.Fori(0, NT) as t:
                    p.sp(sp, t)
            p.sp_end(sp)

        @block.gpsimd
        def _(pool):
            pool.memset(summand[:, :, D:W1], 1.0).then_inc(ones_ready, 1)
            if weighted:
                pool.memset(m.acc[:], 0.0).then_inc(ones_ready, 1)
            with pool.Fori(0, GROUPS) as j:
                for q in range(NQ):
                    pool.wait_ge(ix_ready, j * NQ + q + 1)
                    pool.nop(nofuse=True)
                    for i in range(QUAD):
                        k = q * QUAD + i
                        pool.indirect_dma_start(out=rows[:, k, 0:D], out_offset=None, in_=table,
                                                in_offset=bass.IndirectOffsetOnAxis(ap=ix[:, k:k + 1], axis=0)
                                                ).then_inc(gathered[q], 16)

        @block.scalar
        def _(act):
            def next_ix(j, q):
                act.wait_ge(summed, NQ + j * NQ + q + 1)
                act.nop(nofuse=True)
                nc.scalar.activation(ix[:, q * QUAD:(q + 1) * QUAD],
                                     m.items[:, idx_row, ds((j + 1) * SLOTS + q * QUAD, QUAD)], ACT.Copy).then_inc(ix_ready, 1)

            def group(j):
                for q in range(NQ):
                    if edge_mlp:
                        act.wait_ge(msg_ps, j * NQ + q + 1)
                        nc.scalar.activation(msg[:, q * QUAD:(q + 1) * QUAD, 0:D],
                                             ps_msg[:, q % 2, :].rearrange("p (i f) -> p i f", i=QUAD), ACT.Relu).then_inc(msg_ready, 1)
                        if q:
                            next_ix(j, q - 1)
                    else:
                        next_ix(j, q)
                if edge_mlp:
                    next_ix(j, NQ - 1)

            for q in range(NQ):
                nc.scalar.activation(ix[:, q * QUAD:(q + 1) * QUAD], m.items[:, idx_row, q * QUAD:(q + 1) * QUAD],
                                     ACT.Copy).then_inc(ix_ready, 1)
            over_tiles(act, group, lambda t: p.act(act, t))

        @block.vector
        def _(dve):
            v = nc.vector
            iota = m.consts[:, C_IOTA:C_IOTA + P].unsqueeze(1).to_broadcast([P, QUAD, P])

            def group(j):
                for q in range(NQ):
                    t = j * NQ + q
                    k0 = j * SLOTS + q * QUAD
                    o = oh[:, q * QUAD:(q + 1) * QUAD, :]
                    dve.wait_ge(summed, t + 1)
                    dloc = m.items[:, 1, ds(k0, QUAD)].unsqueeze(2).to_broadcast([P, QUAD, P])
                    if weighted:
                        w = m.items[:, 2, ds(k0, QUAD)].unsqueeze(2).to_broadcast([P, QUAD, P])
                        v.tensor_tensor(o, iota, dloc, ALU.is_equal).then_inc(oh_eq, 1)
                        dve.wait_ge(oh_eq, t + 1)
                        v.tensor_tensor(o, o, w, ALU.mult).then_inc(oh_ready, 1)
                    else:
                        v.tensor_tensor(o, iota, dloc, ALU.is_equal).then_inc(oh_ready, 1)
                    tiles = load4(nc, mybir.EngineType.DVE, m.item_tc[0:1, ds(k0, QUAD)], NT - 1)
                    dve.wait_ge(summed, NQ + t + 1)
                    for i in range(QUAD):
                        a = m.acc[:, ds(tiles[i], 1), :].rearrange("p a f -> p (a f)")
                        dve.wait_ge(added, QUAD * t + 2 * QUAD + i)
                        v.tensor_tensor(a, a, sums[:, 2 * (q % 2) + i // 2, (i % 2) * W1:(i % 2 + 1) * W1],
                                        ALU.add).then_inc(added, 1)
                dve.wait_ge(added, QUAD * t + 3 * QUAD)

            dve.wait_ge(ones_ready, 2 if weighted else 1)
            over_tiles(dve, group, lambda t: p.dve(dve, t))

        @block.tensor
        def _(pe):
            ident = m.consts[:, C_ID:C_ID + P]

            def group(j):
                for q in range(NQ):
                    t = j * NQ + q
                    pe.wait_ge(gathered[q], (j + 1) * (QUAD * 16))
                    if edge_mlp:
                        pe.wait_ge(attr_in[q], (j + 1) * (QUAD * 16))
                        pe.wait_ge(msg_ready, t + 1)
                        for i in range(QUAD):
                            k = q * QUAD + i
                            o = ps_msg[:, q % 2, i * P:(i + 1) * P]
                            nc.tensor.matmul(o, attr[:, k, :], m.wmsg[:, 1, :], start=True, stop=False)
                            last = nc.tensor.matmul(o, ident, rows[:, k, 0:D], start=False, stop=True)
                        last.then_inc(msg_ps, 1)
                        pe.wait_ge(msg_ready, 2 + t + 1)
                    pe.wait_ge(oh_ready, t + 1)
                    pe.wait_ge(added, QUAD * t + QUAD)
                    for i in range(QUAD):
                        k = q * QUAD + i
                        last = nc.tensor.matmul(sums[:, 2 * (q % 2) + i // 2, (i % 2) * W1:(i % 2 + 1) * W1],
                                                oh[:, k, :], summand[:, k, :], start=True, stop=True)
                    last.then_inc(summed, 1)

            pe.wait_ge(ones_ready, 1)
            over_tiles(pe, group, lambda t: p.pe(pe, t))


def norm(nc, c, y, stats, mv, var_ready, sd, sd_ready, count, rs, out):
    v = nc.vector
    c.link(v.bn_stats(stats, y))
    c.eng.nop(nofuse=True)
    v.bn_aggr(mv, stats).then_inc(var_ready, 1)
    c.eng.wait_ge(sd_ready, count)
    c.link(v.reciprocal(rs, sd))
    return v.tensor_scalar(out, y, mv[:, 0:1], rs, op0=ALU.subtract, op1=ALU.mult)


def gru_tile(nc, m, d, s):
    v, te, ac = nc.vector, nc.tensor, nc.scalar
    b4, b5, b6, b7 = s.bank
    tb = s.sb("tb", [P, NTAB, W1])
    rev = s.sb("rev", [P, W1])
    ws, safe, inv = s.sb("ws", [P, 2]), s.sb("safe", [P, 2]), s.sb("inv", [P, 2])
    nb, nbT = s.sb("nb", [P, 3 * D]), s.sb("nbT", [P, 3 * P])
    rz, u, nn, y = s.sb("rz", [P, 2 * D]), s.sb("u", [P, D]), s.sb("nn", [P, D]), s.sb("y", [P, D])
    stats, mv, sd, rs = s.sb("stats", [P, 6]), s.sb("mv", [P, 2]), s.sb("sd", [P, 1]), s.sb("rs", [P, 1])
    xs, xT, tout = s.sb("xs", [P, D]), s.sb("xT", [P, P]), s.sb("tout", [P, R * D])
    tab_in, tab_used, nb_ready, nbT_ps, nbT_ready = (s.sem("tab_in"), s.sem("tab_used"), s.sem("nb_ready"),
                                                     s.sem("nbT_ps"), s.sem("nbT_ready"))
    gates, rz_ready, pre_ready, tanh_ready = s.sem("gates"), s.sem("rz_ready"), s.sem("pre_ready"), s.sem("tanh_ready")
    var_ready, sd_ready, x_ready, xT_ps, xT_ready = (s.sem("var_ready"), s.sem("sd_ready"), s.sem("x_ready"),
                                                     s.sem("xT_ps"), s.sem("xT_ready"))
    prod, ev_act, ev_dve, written = s.sem("prod"), s.sem("ev_act"), s.sem("ev_dve"), s.sem("written")
    ident = m.consts[:, C_ID:C_ID + P]
    ident_ones = m.ones[0:1, 0:P]

    def credits(sp):
        sp.sem_inc(tab_used, 1)
        sp.sem_inc(ev_act, 2)
        sp.sem_inc(ev_dve, 3)
        sp.sem_inc(written, 16)

    def sp(sp, t):
        sp.wait_ge(tab_used, t + 1)
        sp.nop(nofuse=True)
        sp.dma_start(tb[:], d["tables"].rearrange("(k n) f -> n k f", k=NTAB)[ds(t * P, P), :, :]).then_inc(tab_in, 16)
        sp.wait_ge(ev_act, (t + 2) * 2)
        sp.nop(nofuse=True)
        sp.wait_ge(ev_dve, (t + 2) * 3)
        sp.nop(nofuse=True)
        sp.dma_start(d["rel_table"].rearrange("(n r) o -> n (r o)", r=R)[ds(t * P, P), :], tout[:]).then_inc(written, 16)

    def sp_end(sp):
        sp.wait_ge(written, 16 * (NT + 1))

    def dve(dve, t):
        c = Chain(dve, s.chain, t, s.steps)
        x, acc = tile_of(m.x, t), tile_of(m.acc, t)
        dve.wait_ge(tab_in, (t + 1) * 16)
        v.tensor_reduce(rev[:], tb[:].rearrange("p k f -> p f k"), AX.X, ALU.add).then_inc(tab_used, 1)
        dve.wait_ge(tab_used, t + 2)
        c.link(v.tensor_scalar_mul(ws[:, 0:1], m.acc[:, ds(t, 1), D:W1].rearrange("p a f -> p (a f)"), 1.0))
        c.link(v.tensor_copy(ws[:, 1:2], rev[:, D:W1]))
        c.link(v.scalar_tensor_tensor(safe[:], ws[:], 0.0, ws[:], ALU.is_le, ALU.add))
        c.link(v.reciprocal(safe[:], safe[:]))
        c.link(v.scalar_tensor_tensor(inv[:], ws[:], 0.0, safe[:], ALU.is_gt, ALU.mult))
        v.tensor_scalar_mul(nb[:, 2 * D:3 * D], x, 1.0).then_inc(nb_ready, 1)
        v.tensor_scalar(nb[:, 0:D], acc, inv[:, 0:1], None, op0=ALU.mult).then_inc(nb_ready, 1)
        v.tensor_scalar(nb[:, D:2 * D], rev[:, 0:D], inv[:, 1:2], None, op0=ALU.mult).then_inc(nb_ready, 1)
        dve.wait_ge(rz_ready, t + 1)
        c.link(v.tensor_tensor(u[:], rz[:, 0:D], b6[:, D:2 * D], ALU.mult))
        v.tensor_tensor(u[:], u[:], b6[:, 0:D], ALU.add).then_inc(pre_ready, 1)
        dve.wait_ge(tanh_ready, t + 1)
        c.link(v.tensor_tensor(y[:], x, nn[:], ALU.subtract))
        c.link(v.tensor_tensor(y[:], y[:], rz[:, D:2 * D], ALU.mult))
        c.link(v.tensor_tensor(y[:], y[:], nn[:], ALU.add))
        c.link(v.tensor_tensor(y[:], y[:], x, ALU.add))
        norm(nc, c, y[:], stats[:], mv[:], var_ready, sd[:], sd_ready, t + 1, rs[:], xs[:]).then_inc(x_ready, 1)
        dve.wait_ge(x_ready, t + 1)
        v.tensor_scalar_mul(x, xs[:], 1.0)
        dve.wait_ge(prod, t * 5 + 1)
        v.tensor_scalar_mul(acc, b6[:, 2 * D:3 * D], 1.0).then_inc(ev_dve, 1)
        v.tensor_scalar_mul(m.acc[:, ds(t, 1), D:W1].rearrange("p a f -> p (a f)"), m.zeros[:, 0:1], 1.0)
        dve.wait_ge(written, (t + 1) * 16)
        dve.wait_ge(prod, t * 5 + 3)
        v.tensor_copy(tout[:, 512:1024], b7[:]).then_inc(ev_dve, 1)
        dve.wait_ge(prod, t * 5 + 5)
        v.tensor_copy(tout[:, 1536:2048], b5[:]).then_inc(ev_dve, 1)
        c.end()

    def act(act, t):
        act.wait_ge(nbT_ps, t + 1)
        ac.activation(nbT[:], b4[:, 0:3 * P], ACT.Copy).then_inc(nbT_ready, 1)
        act.wait_ge(gates, t + 1)
        ac.activation(rz[:], b5[:, 0:2 * D], ACT.Sigmoid).then_inc(rz_ready, 1)
        act.wait_ge(pre_ready, t + 1)
        ac.activation(nn[:], u[:], ACT.Tanh).then_inc(tanh_ready, 1)
        act.wait_ge(var_ready, t + 1)
        ac.activation(sd[:], mv[:, 1:2], ACT.Sqrt, bias=m.eps[:]).then_inc(sd_ready, 1)
        act.wait_ge(xT_ps, t + 1)
        ac.activation(xT[:], b4[:, 0:P], ACT.Copy).then_inc(xT_ready, 1)
        act.wait_ge(written, (t + 1) * 16)
        act.wait_ge(prod, t * 5 + 2)
        ac.activation(tout[:, 0:512], b5[:], ACT.Copy).then_inc(ev_act, 1)
        act.wait_ge(prod, t * 5 + 4)
        ac.activation(tout[:, 1024:1536], b4[:], ACT.Copy).then_inc(ev_act, 1)

    def pe(pe, t):
        pe.wait_ge(nb_ready, (t + 1) * 3)
        pe.wait_ge(ev_act, (t + 1) * 2)
        pe.wait_ge(ev_dve, (t + 1) * 3)
        te.transpose(b4[:, 0:P], nb[:, 0:D], ident)
        te.transpose(b4[:, P:2 * P], nb[:, D:2 * D], ident)
        te.transpose(b4[:, 2 * P:3 * P], nb[:, 2 * D:3 * D], ident).then_inc(nbT_ps, 1)
        pe.wait_ge(nbT_ready, t + 1)
        n1, n2, xt = nbT[:, 0:P], nbT[:, P:2 * P], nbT[:, 2 * P:3 * P]
        te.matmul(b5[:, 0:2 * D], ident_ones, m.b_ih[:, 0:2 * D], start=True, stop=False)
        te.matmul(b5[:, 0:2 * D], ident_ones, m.b_hh[:, 0:2 * D], start=False, stop=False)
        te.matmul(b5[:, 0:2 * D], n1, m.fold[:, 0, 0:2 * D], start=False, stop=False)
        te.matmul(b5[:, 0:2 * D], n2, m.fold[:, 1, 0:2 * D], start=False, stop=False)
        te.matmul(b5[:, 0:2 * D], xt, m.whh[:, 0:2 * D], start=False, stop=True)
        te.matmul(b6[:, 0:D], ident_ones, m.b_ih[:, 2 * D:3 * D], start=True, stop=False)
        te.matmul(b6[:, 0:D], n1, m.fold[:, 0, 2 * D:3 * D], start=False, stop=False)
        te.matmul(b6[:, 0:D], n2, m.fold[:, 1, 2 * D:3 * D], start=False, stop=True)
        te.matmul(b6[:, D:2 * D], ident_ones, m.b_hh[:, 2 * D:3 * D], start=True, stop=False)
        te.matmul(b6[:, D:2 * D], xt, m.whh[:, 2 * D:3 * D], start=False, stop=True).then_inc(gates, 1)
        pe.wait_ge(x_ready, t + 1)
        te.transpose(b4[:, 0:P], xs[:], ident).then_inc(xT_ps, 1)
        pe.wait_ge(xT_ready, t + 1)
        te.matmul(b6[:, 2 * D:3 * D], ident_ones, m.b1[:], start=True, stop=False)
        te.matmul(b6[:, 2 * D:3 * D], xT[:], m.selfw[:], start=False, stop=True).then_inc(prod, 1)
        for i, bank in enumerate((b5, b7, b4, b5)):
            if i == 3:
                pe.wait_ge(ev_act, t * 2 + 3)
            te.matmul(bank[:], xT[:], m.rel[:, i * 512:(i + 1) * 512], start=True, stop=True).then_inc(prod, 1)

    return TileProgram(credits=credits, sp=sp, sp_end=sp_end, dve=dve, act=act, pe=pe)


def rgcn_tile(nc, m, d, s):
    v, te, ac = nc.vector, nc.tensor, nc.scalar
    b4, b5 = s.bank
    xs, deg = s.sb("xs", [P, D]), s.sb("deg", [P, 1])
    y, xT, out = s.sb("y", [P, D]), s.sb("xT", [P, P]), s.sb("out", [P, D])
    stats, mv, sd, rs = s.sb("stats", [P, 6]), s.sb("mv", [P, 2]), s.sb("sd", [P, 1]), s.sb("rs", [P, 1])
    var_ready, sd_ready, x_ready, xT_ps, xT_ready = (s.sem("var_ready"), s.sem("sd_ready"), s.sem("x_ready"),
                                                     s.sem("xT_ps"), s.sem("xT_ready"))
    prod, out_ready, written = s.sem("prod"), s.sem("out_ready"), s.sem("written")
    ident = m.consts[:, C_ID:C_ID + P]

    def credits(sp):
        sp.sem_inc(written, 16)

    def sp(sp, t):
        sp.wait_ge(out_ready, t + 1)
        sp.nop(nofuse=True)
        sp.dma_start(d["msg_table"][ds(t * P, P), :], out[:]).then_inc(written, 16)

    def sp_end(sp):
        sp.wait_ge(written, 16 * (NT + 1))

    def dve(dve, t):
        c = Chain(dve, s.chain, t, s.steps)
        x, acc = tile_of(m.x, t), tile_of(m.acc, t)
        c.link(v.tensor_scalar_max(deg[:], m.acc[:, ds(t, 1), D:W1].rearrange("p a f -> p (a f)"), 1.0))
        c.link(v.reciprocal(deg[:], deg[:]))
        v.tensor_scalar_mul(m.inv_deg[:, ds(t, 1)], deg[:], 1.0)
        c.link(v.scalar_tensor_tensor(y[:], acc, 0.0, x, ALU.max, ALU.add))
        c.link(v.tensor_scalar_mul(tile_of(m.acc, t, W1), m.zeros[:], 1.0))
        norm(nc, c, y[:], stats[:], mv[:], var_ready, sd[:], sd_ready, t + 1, rs[:], xs[:]).then_inc(x_ready, 1)
        dve.wait_ge(x_ready, t + 1)
        v.tensor_scalar_mul(x, xs[:], 1.0)
        c.end()

    def act(act, t):
        act.wait_ge(var_ready, t + 1)
        ac.activation(sd[:], mv[:, 1:2], ACT.Sqrt, bias=m.eps[:]).then_inc(sd_ready, 1)
        act.wait_ge(xT_ps, t + 1)
        ac.activation(xT[:], b4[:, 0:P], ACT.Copy).then_inc(xT_ready, 1)
        act.wait_ge(prod, t + 1)
        act.wait_ge(written, (t + 1) * 16)
        ac.activation(out[:], b5[:, 0:D], ACT.Copy).then_inc(out_ready, 1)

    def pe(pe, t):
        pe.wait_ge(x_ready, t + 1)
        te.transpose(b4[:, 0:P], xs[:], ident).then_inc(xT_ps, 1)
        pe.wait_ge(xT_ready, t + 1)
        te.matmul(b5[:, 0:D], m.ones[0:1, 0:P], m.b_msg[:], start=True, stop=False)
        te.matmul(b5[:, 0:D], xT[:], m.wmsg[:, 0, :], start=False, stop=True).then_inc(prod, 1)

    return TileProgram(credits=credits, sp=sp, sp_end=sp_end, dve=dve, act=act, pe=pe)


def mlp_tile(nc, m, d, s):
    v, te, ac = nc.vector, nc.tensor, nc.scalar
    b4, b5 = s.bank
    xs = s.sb("xs", [P, D])
    y, mx, mxT = s.sb("y", [P, D]), s.sb("mx", [P, 2 * D]), s.sb("mxT", [P, 2 * P])
    stats, mv, sd, rs = s.sb("stats", [P, 6]), s.sb("mv", [P, 2]), s.sb("sd", [P, 1]), s.sb("rs", [P, 1])
    var_ready, sd_ready, x_ready, mean_ready, mxT_ps, mxT_ready = (
        s.sem("var_ready"), s.sem("sd_ready"), s.sem("x_ready"), s.sem("mean_ready"), s.sem("mxT_ps"), s.sem("mxT_ready"))
    prod, written = s.sem("prod"), s.sem("written")
    ident = m.consts[:, C_ID:C_ID + P]

    def credits(sp):
        sp.sem_inc(written, 16)

    def sp(sp, t):
        pass

    def sp_end(sp):
        sp.wait_ge(written, 16 * (NT + 1))

    def dve(dve, t):
        c = Chain(dve, s.chain, t, s.steps)
        x, acc = tile_of(m.x, t), tile_of(m.acc, t)
        v.tensor_scalar_mul(mx[:, D:2 * D], x, 1.0).then_inc(mean_ready, 1)
        v.tensor_scalar(mx[:, 0:D], acc, m.inv_deg[:, ds(t, 1)], None, op0=ALU.mult).then_inc(mean_ready, 1)
        dve.wait_ge(mean_ready, (t + 1) * 2)
        c.link(v.tensor_scalar_mul(tile_of(m.acc, t, W1), m.zeros[:], 1.0))
        dve.wait_ge(prod, t + 1)
        c.link(norm(nc, c, b5[:, 0:D], stats[:], mv[:], var_ready, sd[:], sd_ready, t * 2 + 1, rs[:], y[:]))
        c.link(v.tensor_tensor(y[:], y[:], m.gamma[:], ALU.mult))
        c.link(v.tensor_tensor(y[:], y[:], m.beta[:], ALU.add))
        c.link(v.tensor_tensor(y[:], y[:], x, ALU.add))
        c.link(v.scalar_tensor_tensor(y[:], y[:], 0.0, x, ALU.max, ALU.add))
        dve.wait_ge(written, (t + 1) * 16)
        norm(nc, c, y[:], stats[:], mv[:], var_ready, sd[:], sd_ready, t * 2 + 2, rs[:], xs[:]).then_inc(x_ready, 1)
        dve.wait_ge(x_ready, t + 1)
        v.tensor_scalar_mul(x, xs[:], 1.0)
        c.end()

    def act(act, t):
        act.wait_ge(mxT_ps, t + 1)
        ac.activation(mxT[:], b4[:, 0:2 * P], ACT.Copy).then_inc(mxT_ready, 1)
        for i in range(2):
            act.wait_ge(var_ready, t * 2 + i + 1)
            ac.activation(sd[:], mv[:, 1:2], ACT.Sqrt, bias=m.eps[:]).then_inc(sd_ready, 1)
        act.wait_ge(x_ready, t + 1)
        act.nop(nofuse=True)
        act.dma_start(d["x3_table"][ds(t * P, P), :], xs[:]).then_inc(written, 16)

    def pe(pe, t):
        pe.wait_ge(mean_ready, (t + 1) * 2)
        te.transpose(b4[:, 0:P], mx[:, 0:D], ident)
        te.transpose(b4[:, P:2 * P], mx[:, D:2 * D], ident).then_inc(mxT_ps, 1)
        pe.wait_ge(mxT_ready, t + 1)
        te.matmul(b5[:, 0:D], m.ones[0:1, 0:P], m.b_upd[:], start=True, stop=False)
        te.matmul(b5[:, 0:D], mxT[:, P:2 * P], m.wupd[:, 0, :], start=False, stop=False)
        te.matmul(b5[:, 0:D], mxT[:, 0:P], m.wupd[:, 1, :], start=False, stop=True).then_inc(prod, 1)

    return TileProgram(credits=credits, sp=sp, sp_end=sp_end, dve=dve, act=act, pe=pe)


def sage1_tile(nc, m, d, s):
    v, te, ac = nc.vector, nc.tensor, nc.scalar
    b4, b5, b6, b7 = s.bank
    mx, mxT, h, hT = s.sb("mx", [P, 2 * D]), s.sb("mxT", [P, 2 * P]), s.sb("h", [P, D]), s.sb("hT", [P, P])
    mean_ready, mxT_ps, mxT_ready, prod, h_ready, hT_ps, hT_ready, own, x_ready, written = (
        s.sem("mean_ready"), s.sem("mxT_ps"), s.sem("mxT_ready"), s.sem("prod"), s.sem("h_ready"), s.sem("hT_ps"),
        s.sem("hT_ready"), s.sem("own"), s.sem("x_ready"), s.sem("written"))
    ident = m.consts[:, C_ID:C_ID + P]

    def credits(sp):
        sp.sem_inc(written, 16)

    def sp(sp, t):
        sp.wait_ge(h_ready, t + 1)
        sp.nop(nofuse=True)
        sp.dma_start(d["h_table"][ds(t * P, P), :], h[:]).then_inc(written, 16)

    def sp_end(sp):
        sp.wait_ge(written, 16 * (NT + 1))

    def dve(dve, t):
        c = Chain(dve, s.chain, t, s.steps)
        x, acc = tile_of(m.x, t), tile_of(m.acc, t)
        v.tensor_scalar_mul(mx[:, D:2 * D], x, 1.0).then_inc(mean_ready, 1)
        v.tensor_scalar(mx[:, 0:D], acc, m.inv_deg[:, ds(t, 1)], None, op0=ALU.mult).then_inc(mean_ready, 1)
        dve.wait_ge(mean_ready, (t + 1) * 2)
        c.link(v.tensor_scalar_mul(tile_of(m.acc, t, W1), m.zeros[:], 1.0))
        dve.wait_ge(own, t + 1)
        v.tensor_tensor(x, x, b7[:, 0:D], ALU.add).then_inc(x_ready, 1)
        c.end()

    def act(act, t):
        act.wait_ge(mxT_ps, t + 1)
        ac.activation(mxT[:], b4[:, 0:2 * P], ACT.Copy).then_inc(mxT_ready, 1)
        act.wait_ge(prod, t + 1)
        act.wait_ge(written, (t + 1) * 16)
        ac.activation(h[:], b5[:, 0:D], ACT.Relu).then_inc(h_ready, 1)
        act.wait_ge(hT_ps, t + 1)
        ac.activation(hT[:], b6[:, 0:P], ACT.Copy).then_inc(hT_ready, 1)

    def pe(pe, t):
        pe.wait_ge(mean_ready, (t + 1) * 2)
        te.transpose(b4[:, 0:P], mx[:, 0:D], ident)
        te.transpose(b4[:, P:2 * P], mx[:, D:2 * D], ident).then_inc(mxT_ps, 1)
        pe.wait_ge(mxT_ready, t + 1)
        te.matmul(b5[:, 0:D], m.ones[0:1, 0:P], m.b31[:], start=True, stop=False)
        te.matmul(b5[:, 0:D], mxT[:, 0:P], m.wl1[:], start=False, stop=False)
        te.matmul(b5[:, 0:D], mxT[:, P:2 * P], m.wr1[:], start=False, stop=True).then_inc(prod, 1)
        pe.wait_ge(h_ready, t + 1)
        te.transpose(b6[:, 0:P], h[:], ident).then_inc(hT_ps, 1)
        pe.wait_ge(hT_ready, t + 1)
        te.matmul(b7[:, 0:D], m.ones[0:1, 0:P], m.b32[:], start=True, stop=False)
        te.matmul(b7[:, 0:D], hT[:], m.wr2[:], start=False, stop=True).then_inc(own, 1)

    return TileProgram(credits=credits, sp=sp, sp_end=sp_end, dve=dve, act=act, pe=pe)


def sage2_tile(nc, m, d, s):
    v, te, ac = nc.vector, nc.tensor, nc.scalar
    b4, b5 = s.bank
    y, mean, mT, out = s.sb("y", [P, D]), s.sb("mean", [P, D]), s.sb("mT", [P, P]), s.sb("out", [P, D])
    stats, mv, sd, rs = s.sb("stats", [P, 6]), s.sb("mv", [P, 2]), s.sb("sd", [P, 1]), s.sb("rs", [P, 1])
    var_ready, sd_ready, out_ready, mean_ready, mT_ps, mT_ready = (
        s.sem("var_ready"), s.sem("sd_ready"), s.sem("out_ready"), s.sem("mean_ready"), s.sem("mT_ps"), s.sem("mT_ready"))
    prod, written = s.sem("prod"), s.sem("written")
    ident = m.consts[:, C_ID:C_ID + P]

    def credits(sp):
        sp.sem_inc(written, 16)

    def sp(sp, t):
        sp.wait_ge(out_ready, t + 1)
        sp.nop(nofuse=True)
        sp.dma_start(d["out"][ds(t * P, P), :], out[:]).then_inc(written, 16)

    def sp_end(sp):
        sp.wait_ge(written, 16 * (NT + 1))

    def dve(dve, t):
        c = Chain(dve, s.chain, t, s.steps)
        x, acc = tile_of(m.x, t), tile_of(m.acc, t)
        v.tensor_scalar(mean[:], acc, m.inv_deg[:, ds(t, 1)], None, op0=ALU.mult).then_inc(mean_ready, 1)
        dve.wait_ge(prod, t + 1)
        c.link(v.tensor_tensor(y[:], x, b5[:, 0:D], ALU.add))
        dve.wait_ge(written, (t + 1) * 16)
        norm(nc, c, y[:], stats[:], mv[:], var_ready, sd[:], sd_ready, t + 1, rs[:], out[:]).then_inc(out_ready, 1)
        c.end()

    def act(act, t):
        act.wait_ge(mT_ps, t + 1)
        ac.activation(mT[:], b4[:, 0:P], ACT.Copy).then_inc(mT_ready, 1)
        act.wait_ge(var_ready, t + 1)
        ac.activation(sd[:], mv[:, 1:2], ACT.Sqrt, bias=m.eps[:]).then_inc(sd_ready, 1)

    def pe(pe, t):
        pe.wait_ge(mean_ready, t + 1)
        te.transpose(b4[:, 0:P], mean[:], ident).then_inc(mT_ps, 1)
        pe.wait_ge(mT_ready, t + 1)
        te.matmul(b5[:, 0:D], mT[:], m.wl2[:], start=True, stop=True).then_inc(prod, 1)

    return TileProgram(credits=credits, sp=sp, sp_end=sp_end, dve=dve, act=act, pe=pe)



def program(nc, d):
    with ExitStack() as ctx:
        def sb(name, shape, dt=F32):
            return ctx.enter_context(nc.sbuf_tensor(name, shape, dt))

        m = Memory()
        m.x = sb("x", [P, NT, W1])
        m.items = sb("items", [P, 4, ITEMS + SLOTS])
        m.item_tc = sb("item_tc", [1, 2 * ITEMS], I32)
        m.tile_steps = sb("tile_steps", [1, NT + 1], I32)
        m.inv_deg = sb("inv_deg", [P, NT])
        m.consts = sb("consts", [P, C_W])
        m.ones = sb("ones", [1, P])
        m.zeros = sb("zeros", [P, W1])
        m.eps = sb("eps", [P, 1])
        m.fold = sb("fold", [P, 2, 3 * D])
        m.whh = sb("whh", [P, 3 * D])
        m.b_ih, m.b_hh = sb("b_ih", [1, 3 * D]), sb("b_hh", [1, 3 * D])
        m.rel = sb("rel", [P, R * D])
        m.selfw, m.b1 = sb("selfw", [P, D]), sb("b1", [1, D])
        m.wmsg, m.b_msg = sb("wmsg", [P, 2, D]), sb("b_msg", [1, D])
        m.wupd, m.b_upd = sb("wupd", [P, 2, D]), sb("b_upd", [1, D])
        m.gamma, m.beta = sb("gamma", [P, D]), sb("beta", [P, D])
        m.wl1, m.wr1, m.b31 = sb("wl1", [P, D]), sb("wr1", [P, D]), sb("b31", [1, D])
        m.wl2, m.wr2, m.b32 = sb("wl2", [P, D]), sb("wr2", [P, D]), sb("b32", [1, D])

        plan_phase(nc, m, d)
        scatter_phase(nc, m, d)
        m.acc = sb("acc", [P, NT, W1])
        layer_phase(nc, m, d, "gru", d["x_pad"], 0, True, False, 4, 12, gru_tile)
        layer_phase(nc, m, d, "rgcn", d["rel_table"], 3, False, False, 2, 6, rgcn_tile)
        layer_phase(nc, m, d, "mlp", d["msg_table"], 0, False, True, 2, 10, mlp_tile)
        layer_phase(nc, m, d, "hop1", d["x3_table"], 0, False, False, 4, 1, sage1_tile)
        layer_phase(nc, m, d, "hop2", d["h_table"], 0, False, False, 2, 3, sage2_tile)


def kernel(**inputs):
    import concourse.bacc as bacc
    from concourse.bass_utils import run_bass_kernel_spmd as run

    a = {k: np.asarray(v) for k, v in inputs.items()}
    slots = (NC + 1) * P

    def padded(v, n, fill):
        out = np.full((n,) + v.shape[1:], fill, v.dtype)
        out[:v.shape[0]] = v
        return out

    src = padded(a["src"], slots, 0).reshape(NC + 1, P)
    dst = padded(a["dst"], slots, NO_NODE).reshape(NC + 1, P)
    typ = padded(a["edge_type_16"], slots, 0).reshape(NC + 1, P)
    arrays = {
        "x_pad": padded(a["x"], NPAD, 0),
        "first_dst": dst[:, 0].reshape(1, NC + 1),
        "dst_rows": dst,
        "edge_rows": np.concatenate([src, dst, typ], axis=1),
        "weight_rows": padded(a["edge_weight"], slots, 0).reshape(NC + 1, P),
        "attr_t": padded(a["edge_attr_128"], slots, 0).reshape(NC + 1, P, D).transpose(0, 2, 1),
        "consts": constants(),
        "L0_gnn_W1": a["L0_gnn_W1"], "L0_gnn_W2": a["L0_gnn_W2"],
        "w_ih_t": a["L0_gnn_w_ih"].T, "w_hh_t": a["L0_gnn_w_hh"].T,
        "b_ih": a["L0_gnn_b_ih"][None], "b_hh": a["L0_gnn_b_hh"][None],
        "rel_t": a["L1_gnn_relation_weights"].transpose(1, 0, 2).reshape(D, R * D),
        "L1_gnn_self_weight": a["L1_gnn_self_weight"], "L1_bias": a["L1_gnn_bias"][None],
        "L2_gnn_W_msg": a["L2_gnn_W_msg"], "b_msg": a["L2_gnn_b_msg"][None],
        "L2_gnn_W_upd": a["L2_gnn_W_upd"], "b_upd": a["L2_gnn_b_upd"][None],
        "gamma": a["L2_gnn_gamma"][None], "beta": a["L2_gnn_beta"][None],
        "wl1_t": a["L3_gnn_Wl1"].T, "wr1_t": a["L3_gnn_Wr1"].T, "b31": a["L3_gnn_b1"][None],
        "wl2_t": a["L3_gnn_Wl2"].T, "wr2_t": a["L3_gnn_Wr2"].T, "b32": a["L3_gnn_b2"][None],
    }
    arrays = {k: np.ascontiguousarray(v) for k, v in arrays.items()}
    nc = bacc.Bacc("TRN2", target_bir_lowering=False, num_devices=1)
    aps = {k: nc.dram_tensor(f"in_{k}", v.shape, mybir.dt.from_np(v.dtype), kind="ExternalInput").ap() for k, v in arrays.items()}
    d = dict(aps)
    d["out"] = nc.dram_tensor("out", (NPAD, D), F32, kind="ExternalOutput").ap()
    d["tables"] = nc.dram_tensor("tables", (NTAB * TROWS, W1), F32).ap()
    d["rel_table"] = nc.dram_tensor("rel_table", (NPAD * R, D), F32).ap()
    d["msg_table"] = nc.dram_tensor("msg_table", (NPAD, D), F32).ap()
    d["x3_table"] = nc.dram_tensor("x3_table", (NPAD, D), F32).ap()
    d["h_table"] = nc.dram_tensor("h_table", (NPAD, D), F32).ap()
    d["tc_dram"] = nc.dram_tensor("tc_dram", (2 * JC, P), I32).ap()
    program(nc, d)
    r = run(nc, [{f"in_{k}": v for k, v in arrays.items()}], core_ids=[0])
    return r.results[0]["out"][:N]
```
